# Optimizing a Trainium2 kernel written in Bass

```python
import numpy as np
import jax
import jax.numpy as jnp

def _softmax(x, axis=-1):
    return jax.nn.softmax(x, axis=axis)

def _gelu(x):
    return jax.nn.gelu(x, approximate=True)

def _silu(x):
    return jax.nn.silu(x)

def _sigmoid(x):
    return jax.nn.sigmoid(x)

def _layernorm(x, axis=-1, eps=1e-05):
    m = jnp.mean(x, axis=axis, keepdims=True)
    v = jnp.var(x, axis=axis, keepdims=True)
    return (x - m) / jnp.sqrt(v + eps)

def _scatter_add(tgt, idx, src, axis=0):
    return tgt.at[idx].add(src)

def _segment_sum(src, seg, n):
    return jax.ops.segment_sum(src, seg, n)
kernel_name = 'mk_dlrm_tower_d1_rec_r8_d1d704'

def setup_inputs(seed: int=0):
    np.random.seed(seed)
    _w = jnp.asarray

    def _rec_inputs():
        import jax
        import jax.numpy as jnp
        _tk = jax.random.key(seed)
        dense_ctx = jax.random.normal(jax.random.fold_in(_tk, 190), (1024, 16), jnp.float32)
        ids = jnp.stack([jax.random.randint(jax.random.fold_in(_tk, 200 + f), (1024,), 0, v, jnp.int32) for f, v in enumerate([1250, 12500, 1250, 12500, 12500, 12500, 125000, 1000, 1250, 12500, 1000, 1000, 125000, 1250, 12500, 125000, 12500, 1250, 12500, 1000, 12500, 1250, 125000, 1000, 1250, 125000, 1250, 12500, 12500, 125000, 12500, 12500, 12500, 1000, 1250, 1000, 1250, 1250, 12500])], axis=1)
        tbl_0 = 0.05 * jax.random.normal(jax.random.fold_in(_tk, 500 + 0), (1250, 16), jnp.float32)
        tbl_1 = 0.05 * jax.random.normal(jax.random.fold_in(_tk, 500 + 1), (12500, 16), jnp.float32)
        tbl_2 = 0.05 * jax.random.normal(jax.random.fold_in(_tk, 500 + 2), (1250, 16), jnp.float32)
        tbl_3 = 0.05 * jax.random.normal(jax.random.fold_in(_tk, 500 + 3), (12500, 16), jnp.float32)
        tbl_4 = 0.05 * jax.random.normal(jax.random.fold_in(_tk, 500 + 4), (12500, 16), jnp.float32)
        tbl_5 = 0.05 * jax.random.normal(jax.random.fold_in(_tk, 500 + 5), (12500, 16), jnp.float32)
        tbl_6 = 0.05 * jax.random.normal(jax.random.fold_in(_tk, 500 + 6), (125000, 16), jnp.float32)
        tbl_7 = 0.05 * jax.random.normal(jax.random.fold_in(_tk, 500 + 7), (1000, 16), jnp.float32)
        tbl_8 = 0.05 * jax.random.normal(jax.random.fold_in(_tk, 500 + 8), (1250, 16), jnp.float32)
        tbl_9 = 0.05 * jax.random.normal(jax.random.fold_in(_tk, 500 + 9), (12500, 16), jnp.float32)
        tbl_10 = 0.05 * jax.random.normal(jax.random.fold_in(_tk, 500 + 10), (1000, 16), jnp.float32)
        tbl_11 = 0.05 * jax.random.normal(jax.random.fold_in(_tk, 500 + 11), (1000, 16), jnp.float32)
        tbl_12 = 0.05 * jax.random.normal(jax.random.fold_in(_tk, 500 + 12), (125000, 16), jnp.float32)
        tbl_13 = 0.05 * jax.random.normal(jax.random.fold_in(_tk, 500 + 13), (1250, 16), jnp.float32)
        tbl_14 = 0.05 * jax.random.normal(jax.random.fold_in(_tk, 500 + 14), (12500, 16), jnp.float32)
        tbl_15 = 0.05 * jax.random.normal(jax.random.fold_in(_tk, 500 + 15), (125000, 16), jnp.float32)
        tbl_16 = 0.05 * jax.random.normal(jax.random.fold_in(_tk, 500 + 16), (12500, 16), jnp.float32)
        tbl_17 = 0.05 * jax.random.normal(jax.random.fold_in(_tk, 500 + 17), (1250, 16), jnp.float32)
        tbl_18 = 0.05 * jax.random.normal(jax.random.fold_in(_tk, 500 + 18), (12500, 16), jnp.float32)
        tbl_19 = 0.05 * jax.random.normal(jax.random.fold_in(_tk, 500 + 19), (1000, 16), jnp.float32)
        tbl_20 = 0.05 * jax.random.normal(jax.random.fold_in(_tk, 500 + 20), (12500, 16), jnp.float32)
        tbl_21 = 0.05 * jax.random.normal(jax.random.fold_in(_tk, 500 + 21), (1250, 16), jnp.float32)
        tbl_22 = 0.05 * jax.random.normal(jax.random.fold_in(_tk, 500 + 22), (125000, 16), jnp.float32)
        tbl_23 = 0.05 * jax.random.normal(jax.random.fold_in(_tk, 500 + 23), (1000, 16), jnp.float32)
        tbl_24 = 0.05 * jax.random.normal(jax.random.fold_in(_tk, 500 + 24), (1250, 16), jnp.float32)
        tbl_25 = 0.05 * jax.random.normal(jax.random.fold_in(_tk, 500 + 25), (125000, 16), jnp.float32)
        tbl_26 = 0.05 * jax.random.normal(jax.random.fold_in(_tk, 500 + 26), (1250, 16), jnp.float32)
        tbl_27 = 0.05 * jax.random.normal(jax.random.fold_in(_tk, 500 + 27), (12500, 16), jnp.float32)
        tbl_28 = 0.05 * jax.random.normal(jax.random.fold_in(_tk, 500 + 28), (12500, 16), jnp.float32)
        tbl_29 = 0.05 * jax.random.normal(jax.random.fold_in(_tk, 500 + 29), (125000, 16), jnp.float32)
        tbl_30 = 0.05 * jax.random.normal(jax.random.fold_in(_tk, 500 + 30), (12500, 16), jnp.float32)
        tbl_31 = 0.05 * jax.random.normal(jax.random.fold_in(_tk, 500 + 31), (12500, 16), jnp.float32)
        tbl_32 = 0.05 * jax.random.normal(jax.random.fold_in(_tk, 500 + 32), (12500, 16), jnp.float32)
        tbl_33 = 0.05 * jax.random.normal(jax.random.fold_in(_tk, 500 + 33), (1000, 16), jnp.float32)
        tbl_34 = 0.05 * jax.random.normal(jax.random.fold_in(_tk, 500 + 34), (1250, 16), jnp.float32)
        tbl_35 = 0.05 * jax.random.normal(jax.random.fold_in(_tk, 500 + 35), (1000, 16), jnp.float32)
        tbl_36 = 0.05 * jax.random.normal(jax.random.fold_in(_tk, 500 + 36), (1250, 16), jnp.float32)
        tbl_37 = 0.05 * jax.random.normal(jax.random.fold_in(_tk, 500 + 37), (1250, 16), jnp.float32)
        tbl_38 = 0.05 * jax.random.normal(jax.random.fold_in(_tk, 500 + 38), (12500, 16), jnp.float32)
        _rk = jax.random.fold_in(_tk, 7)
        W_top1 = 0.0606339 * jax.random.normal(jax.random.fold_in(_tk, 801), (272, 512), jnp.float32)
        W_top2 = 0.0441942 * jax.random.normal(jax.random.fold_in(_tk, 802), (512, 256), jnp.float32)
        W_top3 = 0.0625 * jax.random.normal(jax.random.fold_in(_tk, 803), (256, 1), jnp.float32)
        b_top1 = jnp.zeros((512,), jnp.float32)
        b_top2 = jnp.zeros((256,), jnp.float32)
        return (dense_ctx, ids, tbl_0, tbl_1, tbl_2, tbl_3, tbl_4, tbl_5, tbl_6, tbl_7, tbl_8, tbl_9, tbl_10, tbl_11, tbl_12, tbl_13, tbl_14, tbl_15, tbl_16, tbl_17, tbl_18, tbl_19, tbl_20, tbl_21, tbl_22, tbl_23, tbl_24, tbl_25, tbl_26, tbl_27, tbl_28, tbl_29, tbl_30, tbl_31, tbl_32, tbl_33, tbl_34, tbl_35, tbl_36, tbl_37, tbl_38, W_top1, b_top1, W_top2, b_top2, W_top3)
    dense_ctx, ids, tbl_0, tbl_1, tbl_2, tbl_3, tbl_4, tbl_5, tbl_6, tbl_7, tbl_8, tbl_9, tbl_10, tbl_11, tbl_12, tbl_13, tbl_14, tbl_15, tbl_16, tbl_17, tbl_18, tbl_19, tbl_20, tbl_21, tbl_22, tbl_23, tbl_24, tbl_25, tbl_26, tbl_27, tbl_28, tbl_29, tbl_30, tbl_31, tbl_32, tbl_33, tbl_34, tbl_35, tbl_36, tbl_37, tbl_38, W_top1, b_top1, W_top2, b_top2, W_top3 = _rec_inputs()

    def _L0_rec_setup():
        import jax, jax.numpy as jnp
        import numpy as np
        B, M, D = (1024, 39, 16)
        S1, S2 = (128, 128)

        def _cin_layer(x0, xk, W, b):
            out = jnp.einsum('bhd,bmd,shm->bsd', xk, x0, W) + b[None, :, None]
            return jax.nn.relu(out)
        key = jax.random.key(seed)
        k0, k1, k2 = jax.random.split(key, 3)
        x0 = jax.random.normal(k0, (B, M, D), dtype=jnp.float32)
        W1 = jax.random.normal(k1, (S1, M, M), dtype=jnp.float32) * 0.05
        b1 = jnp.zeros((S1,), dtype=jnp.float32)
        W2 = jax.random.normal(k2, (S2, S1, M), dtype=jnp.float32) * 0.05
        b2 = jnp.zeros((S2,), dtype=jnp.float32)
        return {'x0': x0, 'W1': W1, 'b1': b1, 'W2': W2, 'b2': b2}
    _L0_rec_all = _L0_rec_setup()
    _L0_rec_in = {k: v for k, v in _L0_rec_all.items() if k in ('W1', 'b1', 'W2', 'b2')}
    del _L0_rec_all
    return {'dense_ctx': dense_ctx, 'ids': ids, 'tbl_0': tbl_0, 'tbl_1': tbl_1, 'tbl_2': tbl_2, 'tbl_3': tbl_3, 'tbl_4': tbl_4, 'tbl_5': tbl_5, 'tbl_6': tbl_6, 'tbl_7': tbl_7, 'tbl_8': tbl_8, 'tbl_9': tbl_9, 'tbl_10': tbl_10, 'tbl_11': tbl_11, 'tbl_12': tbl_12, 'tbl_13': tbl_13, 'tbl_14': tbl_14, 'tbl_15': tbl_15, 'tbl_16': tbl_16, 'tbl_17': tbl_17, 'tbl_18': tbl_18, 'tbl_19': tbl_19, 'tbl_20': tbl_20, 'tbl_21': tbl_21, 'tbl_22': tbl_22, 'tbl_23': tbl_23, 'tbl_24': tbl_24, 'tbl_25': tbl_25, 'tbl_26': tbl_26, 'tbl_27': tbl_27, 'tbl_28': tbl_28, 'tbl_29': tbl_29, 'tbl_30': tbl_30, 'tbl_31': tbl_31, 'tbl_32': tbl_32, 'tbl_33': tbl_33, 'tbl_34': tbl_34, 'tbl_35': tbl_35, 'tbl_36': tbl_36, 'tbl_37': tbl_37, 'tbl_38': tbl_38, 'W_top1': W_top1, 'b_top1': b_top1, 'W_top2': W_top2, 'b_top2': b_top2, 'W_top3': W_top3, 'L0_rec_W1': _L0_rec_in['W1'], 'L0_rec_b1': _L0_rec_in['b1'], 'L0_rec_W2': _L0_rec_in['W2'], 'L0_rec_b2': _L0_rec_in['b2']}

def reference(dense_ctx, ids, tbl_0, tbl_1, tbl_2, tbl_3, tbl_4, tbl_5, tbl_6, tbl_7, tbl_8, tbl_9, tbl_10, tbl_11, tbl_12, tbl_13, tbl_14, tbl_15, tbl_16, tbl_17, tbl_18, tbl_19, tbl_20, tbl_21, tbl_22, tbl_23, tbl_24, tbl_25, tbl_26, tbl_27, tbl_28, tbl_29, tbl_30, tbl_31, tbl_32, tbl_33, tbl_34, tbl_35, tbl_36, tbl_37, tbl_38, W_top1, b_top1, W_top2, b_top2, W_top3, L0_rec_W1, L0_rec_b1, L0_rec_W2, L0_rec_b2):
    import jax
    import jax.numpy as jnp

    def _L0_rec_ref(x0, W1, b1, W2, b2):
        import jax, jax.numpy as jnp
        import numpy as np
        B, M, D = (1024, 39, 16)
        S1, S2 = (128, 128)

        def _cin_layer(x0, xk, W, b):
            out = jnp.einsum('bhd,bmd,shm->bsd', xk, x0, W) + b[None, :, None]
            return jax.nn.relu(out)
        x1 = _cin_layer(x0, x0, W1, b1)
        x2 = _cin_layer(x0, x1, W2, b2)
        p1 = x1.sum(axis=-1)
        p2 = x2.sum(axis=-1)
        return jnp.concatenate([p1, p2], axis=-1)
    e = jnp.stack([tbl_0[ids[:, 0]], tbl_1[ids[:, 1]], tbl_2[ids[:, 2]], tbl_3[ids[:, 3]], tbl_4[ids[:, 4]], tbl_5[ids[:, 5]], tbl_6[ids[:, 6]], tbl_7[ids[:, 7]], tbl_8[ids[:, 8]], tbl_9[ids[:, 9]], tbl_10[ids[:, 10]], tbl_11[ids[:, 11]], tbl_12[ids[:, 12]], tbl_13[ids[:, 13]], tbl_14[ids[:, 14]], tbl_15[ids[:, 15]], tbl_16[ids[:, 16]], tbl_17[ids[:, 17]], tbl_18[ids[:, 18]], tbl_19[ids[:, 19]], tbl_20[ids[:, 20]], tbl_21[ids[:, 21]], tbl_22[ids[:, 22]], tbl_23[ids[:, 23]], tbl_24[ids[:, 24]], tbl_25[ids[:, 25]], tbl_26[ids[:, 26]], tbl_27[ids[:, 27]], tbl_28[ids[:, 28]], tbl_29[ids[:, 29]], tbl_30[ids[:, 30]], tbl_31[ids[:, 31]], tbl_32[ids[:, 32]], tbl_33[ids[:, 33]], tbl_34[ids[:, 34]], tbl_35[ids[:, 35]], tbl_36[ids[:, 36]], tbl_37[ids[:, 37]], tbl_38[ids[:, 38]]], axis=1)
    z = _L0_rec_ref(e, L0_rec_W1, L0_rec_b1, L0_rec_W2, L0_rec_b2)
    z = z.reshape(z.shape[0], -1)
    h = jnp.concatenate([z, dense_ctx], axis=1)
    h = jnp.maximum(h @ W_top1 + b_top1, 0.0)
    h = jnp.maximum(h @ W_top2 + b_top2, 0.0)
    y = h @ W_top3
    return y

_drawn_inputs = setup_inputs


def setup_inputs(seed=0):
    import zlib

    import numpy as np

    out = dict(_drawn_inputs(seed))
    spreads = {'b_top1': (0.0, 0.1),
     'b_top2': (0.0, 0.1),
     'L0_rec_b1': (0.0, 0.1),
     'L0_rec_b2': (0.0, 0.1)}
    factors = {'tbl_0': 4.43,
     'tbl_1': 4.443,
     'tbl_2': 7.059,
     'tbl_3': 6.094,
     'tbl_4': 6.58,
     'tbl_5': 7.216,
     'tbl_6': 5.716,
     'tbl_7': 4.582,
     'tbl_8': 8.0,
     'tbl_9': 7.399,
     'tbl_10': 6.394,
     'tbl_11': 5.723,
     'tbl_12': 5.543,
     'tbl_14': 7.943,
     'tbl_15': 6.608,
     'tbl_16': 7.702,
     'tbl_17': 4.573,
     'tbl_18': 5.412,
     'tbl_19': 4.542,
     'tbl_20': 8.0,
     'tbl_21': 3.351,
     'tbl_22': 8.0,
     'tbl_23': 7.346,
     'tbl_24': 7.604,
     'tbl_25': 5.195,
     'tbl_26': 4.283,
     'tbl_27': 6.252,
     'tbl_28': 8.0,
     'tbl_29': 5.158,
     'tbl_30': 5.124,
     'tbl_31': 3.114,
     'tbl_32': 8.0,
     'tbl_33': 7.338,
     'tbl_34': 7.433,
     'tbl_35': 7.389,
     'tbl_36': 8.0,
     'tbl_37': 8.0,
     'tbl_38': 6.48,
     'tbl_13': 4.159}
    for name, (base, spread) in spreads.items():
        noise = np.random.default_rng([zlib.crc32(name.encode()), seed]).standard_normal(out[name].shape)
        drawn = base * np.exp(spread * noise) if base else spread * noise
        out[name] = jnp.asarray(drawn.astype(out[name].dtype))
    for name, factor in factors.items():
        out[name] = (out[name] * factor).astype(out[name].dtype)
    return out
```

```python
from contextlib import ExitStack

import numpy as np

import concourse.bass as bass
from concourse import mybir
from concourse.alu_op_type import AluOpType as ALU

ACT = mybir.ActivationFunctionType
F32 = mybir.dt.float32
F32R = mybir.dt.float32r
I32 = mybir.dt.int32
AX_X = mybir.AxisListType.X

P = 128
B, M, D = 1024, 39, 16
S = 128
CTX = 16
F1, F2 = 512, 256
BLOCKS = B // P
TILES = 4
DT = D // TILES
N = DT * P
MG, HG = 8, 16
J = -(-M // MG)
G = S // HG
CHUNKS = J * G
UC = 4
UNITS = CHUNKS // UC
SHIFTS = (M + 1) // 2
SC = 3
K1 = SC * M
C1 = -(-SHIFTS // SC)
SEL = J + 1 + C1

KINDS = ["PDPDNPDPDN", "PDPDNPDPDN", "PPDPPPDPPP", "PPDPPPDPPP"]
ZR, HR, LR = 4, 3, 3
LAG = 2
AHEAD_PE, AHEAD_ACT, AHEAD_DVE = 2, 3, 4

BK_B2, BK_ACC2, BK_ACC1, BK_B1, BK_T = (0, 1), (2, 3), 4, (5, 6), 7


def split_count(q, u):
    return sum(c != "N" for c in "".join(KINDS)[: UNITS * q + u])


LAP = "".join(KINDS)
SPLITS, PS, DS = (len(LAP) - LAP.count("N")), LAP.count("P"), LAP.count("D")
NATIVE = sorted({u for k in KINDS for u, c in enumerate(k) if c == "N"})
assert SPLITS % HR == 0 and SPLITS % LR == 0 and len(LAP) % ZR == 0
assert all(k[0] != "N" and k[-1] != "D" for k in KINDS)


def at(i, per, k):
    return (i + 1) * per + k


def cin_tower(nc, tables, ids, w1a, w1b, b1, w2, w2n, b2, sel, ident, wt1, wt1c, bt1, wt2, bt2, wt3, ctx_t, out):
    with ExitStack() as stack:
        def sb(name, shape, dt=F32):
            return stack.enter_context(nc.sbuf_tensor(name, shape, dt))

        def sem(name):
            return stack.enter_context(nc.semaphore(name))

        ps = stack.enter_context(nc.psum_tensor("ps", [P, 8, N], F32))

        ids_all = sb("ids_all", [P, BLOCKS, M], I32)
        ids_now = sb("ids_now", [P, M], I32)
        e_raw = sb("e_raw", [P, M, D])
        e_hl = sb("e_hl", [P, 2 * M, D])
        x0t = sb("x0t", [2 * M, TILES, N], F32R)
        sel_r = sb("sel_r", [2 * M, SEL, P], F32R)
        ident_sb = sb("ident_sb", [P, P])
        w1_sb = sb("w1_sb", [K1, C1, S])
        b1_sb = sb("b1_sb", [S, 1])
        b2_sb = sb("b2_sb", [S, 1])
        w2h = sb("w2h", [P, CHUNKS, S], F32R)
        w2l = sb("w2l", [P, CHUNKS, S], F32R)
        w2n_sb = sb("w2n_sb", [P, len(NATIVE), UC, S])
        a1 = sb("a1", [K1, N])
        z1 = sb("z1", [K1, 2, N])
        x1 = sb("x1", [S, N])
        x2 = sb("x2", [S, N])
        a2 = sb("a2", [P, 2, G, N])
        zr = sb("zr", [P, ZR, UC * N])
        hr = sb("hr", [P, HR, UC * N], F32R)
        lr = sb("lr", [P, LR, UC * N], F32R)
        part1 = sb("part1", [S, TILES, P])
        part2 = sb("part2", [S, TILES, P])
        p1 = sb("p1", [S, B])
        p2 = sb("p2", [S, B])
        bt1_sb = sb("bt1_sb", [P, F1 // P])
        bt2_sb = sb("bt2_sb", [P, F2 // P])
        wt3_sb = sb("wt3_sb", [P, F2 // P])

        zflat = zr[:, :, :].rearrange("p a b -> p (a b)")
        aflat = a2[:, :, :, :].rearrange("p a b c -> p (a b c)")
        w2_stage = zflat[:, 0:CHUNKS * S].rearrange("p (c s) -> p c s", s=S)
        w1b_stage = zflat[0:K1, CHUNKS * S:(CHUNKS + C1) * S].rearrange("p (c s) -> p c s", s=S)
        sel_stage = aflat[0:2 * M, 0:SEL * P].rearrange("p (c s) -> p c s", s=P)
        o = 0
        h1 = zflat[:, o:o + (F1 // P) * B].rearrange("p (c b) -> p c b", b=B)
        o += (F1 // P) * B
        wt1_sb = zflat[:, o:o + 2 * F1].rearrange("p (c f) -> p c f", f=F1)
        o += 2 * F1
        wt1c_sb = zflat[0:CTX, o:o + F1]
        o += F1
        ctx_sb = zflat[0:CTX, o:o + B]
        o += B
        wt2_sb = zflat[:, o:o + (F1 // P) * F2].rearrange("p (c f) -> p c f", f=F2)
        assert o + (F1 // P) * F2 <= ZR * UC * N
        h2 = aflat[:, 0:(F2 // P) * B].rearrange("p (c b) -> p c b", b=B)
        y_sb = aflat[0:1, (F2 // P) * B:(F2 // P) * B + B]

        s_ids = sem("s_ids")
        s_stage = sem("s_stage")
        s_const = sem("s_const")
        s_mlpw = sem("s_mlpw")
        s_now = sem("s_now")
        s_looked = sem("s_looked")
        s_eh = sem("s_eh")
        s_el = sem("s_el")
        s_tr = sem("s_tr")
        s_x0t = sem("s_x0t")
        s_rep1 = sem("s_rep1")
        s_a1 = sem("s_a1")
        s_z1 = sem("s_z1")
        s_mm1 = sem("s_mm1")
        s_x1 = sem("s_x1")
        s_a2 = [sem("s_a2_even"), sem("s_a2_odd")]
        s_p1 = sem("s_p1")
        s_rep2 = sem("s_rep2")
        s_z = sem("s_z")
        s_h = sem("s_h")
        s_lp = sem("s_lp")
        s_ld = sem("s_ld")
        s_hmm = sem("s_hmm")
        s_unit = sem("s_unit")
        s_x2 = sem("s_x2")
        s_p2 = sem("s_p2")
        s_w = sem("s_w")
        s_wl = sem("s_wl")
        s_part = sem("s_part")
        s_mlp = sem("s_mlp")
        s_act = sem("s_act")
        s_out = sem("s_out")

        per_z1, per_rep1, per_rep2, per_u = TILES * C1, TILES * (C1 + 1), TILES * J, TILES * UNITS

        def low_done(i, w):
            lap, w = divmod(w, per_u)
            if LAP[w] == "P":
                return s_lp, at(i, PS, LAP[:w].count("P") + 1 + lap * PS)
            if LAP[w] == "D":
                return s_ld, at(i, DS, LAP[:w].count("D") + 1 + lap * DS)
            return s_unit, at(i, per_u, w + 1 + lap * per_u)

        def unit_of_split(n):
            lap, n = divmod(n, SPLITS)
            return [k for k, c in enumerate(LAP) if c != "N"][n] + lap * per_u

        def credit(eng, pairs):
            for s, n in pairs:
                if n:
                    eng.sem_inc(s, n)

        with nc.Block() as block:
            @block.sync
            def _(sp):
                credit(sp, [(s_a2[0], 16 * G), (s_a2[1], 2 * 16 * G)])
                sp.dma_start(ids_all[:], ids.rearrange("(t p) m -> p t m", p=P)).then_inc(s_ids, 16)
                for dst, src in ((sel_stage, sel), (w2_stage, w2), (w1b_stage, w1b), (w1_sb[:], w1a)):
                    sp.dma_start(dst, src).then_inc(s_stage, 16)
                for dst, src in ((ident_sb[:], ident), (b1_sb[:], b1), (b2_sb[:], b2), (w2n_sb[:], w2n),
                                 (bt1_sb[:], bt1), (bt2_sb[:], bt2), (wt3_sb[:], wt3)):
                    sp.dma_start(dst, src).then_inc(s_const, 16)

                def replicate(i, q):
                    par = (q + 1) % 2
                    sp.wait_ge(s_x1, at(i, TILES, q + 1))
                    for g in range(G):
                        src = x1[g * HG:(g + 1) * HG, :].rearrange("p (o n) -> p o n", o=1)
                        sp.dma_start(a2[:, par, g, :], src.to_broadcast([HG, MG, N])).then_inc(s_a2[par], 16)

                replicate(-1, TILES - 1)
                with sp.Fori(0, BLOCKS - 1) as i:
                    for q in range(TILES):
                        replicate(i, q)
                for q in range(TILES - 1):
                    replicate(BLOCKS - 1, q)
                sp.wait_ge(s_unit, at(BLOCKS - 1, per_u, per_u))
                sp.wait_ge(s_lp, at(BLOCKS - 1, PS, PS))
                for dst, src in ((wt1_sb, wt1), (wt1c_sb, wt1c), (ctx_sb, ctx_t), (wt2_sb, wt2)):
                    sp.dma_start(dst, src).then_inc(s_mlpw, 16)
                sp.wait_ge(s_act, 14)
                sp.dma_start(out, y_sb).then_inc(s_out, 16)
                sp.wait_ge(s_out, 16)

            @block.gpsimd
            def _(pool):
                credit(pool, [(s_lp, PS)])

                def ids_of(k, i):
                    pool.wait_ge(s_looked, at(i, 16 * M, 0))
                    nc.gpsimd.tensor_copy(ids_now[:], ids_all[:, k, :]).then_inc(s_now, 1)
                    pool.wait_ge(s_now, at(i, 1, 1))
                    pool.wait_ge(s_el, at(i, 1, 0))
                    pool.wait_ge(s_eh, at(i, 1, 0))

                def look_up(m):
                    nc.gpsimd.indirect_dma_start(
                        e_raw[:, m, :], None, tables[m], bass.IndirectOffsetOnAxis(ids_now[:, m:m + 1], 0)
                    ).then_inc(s_looked, 16)

                def low(i, q, u):
                    n = split_count(q, u)
                    pool.wait_ge(s_h, at(i, SPLITS, n + 1))
                    pool.wait_ge(s_unit, at(i, per_u, unit_of_split(n - LR) + 1))
                    nc.gpsimd.tensor_tensor(lr[:, n % LR, :], zr[:, (UNITS * q + u) % ZR, :], hr[:, n % HR, :],
                                            ALU.subtract).then_inc(s_lp, 1)

                def tile(i, q, k=None):
                    todo = list(range(M)) if k is not None and q < 2 else []
                    todo = todo[:M // 2] if q == 0 else todo[M // 2:]
                    if todo and q == 0:
                        ids_of(k, i)
                    each = -(-len(todo) // UNITS)
                    for u in range(UNITS):
                        if KINDS[q][u] == "P":
                            low(i, q, u)
                        for m in todo[u * each:(u + 1) * each]:
                            look_up(m)

                pool.wait_ge(s_ids, 16)
                ids_of(0, -1)
                for m in range(M):
                    look_up(m)
                with pool.Fori(0, BLOCKS - 1) as i:
                    for q in range(TILES):
                        tile(i, q, i + 1)
                for q in range(TILES):
                    tile(BLOCKS - 1, q)

            @block.scalar
            def _(act):
                credit(act, [(s_x0t, 2), (s_a1, TILES - 1), (s_x1, TILES - 1), (s_h, SPLITS), (s_x2, TILES)])
                act.wait_ge(s_stage, 4 * 16)
                nc.scalar.activation(sel_r[:], sel_stage, ACT.Copy).then_inc(s_w, 1)
                nc.scalar.activation(w2h[:], w2_stage, ACT.Copy).then_inc(s_w, 1)
                act.wait_ge(s_const, 7 * 16)

                def step(i, q, u, main, nxt, nxt2):
                    if nxt2 and q == 2 and u == 1:
                        act.wait_ge(s_looked, at(i, 16 * M, 16 * M))
                        act.wait_ge(s_tr, at(i, TILES, 2))
                        nc.scalar.activation(e_hl[:, 0:M, :].bitcast(F32R), e_raw[:], ACT.Copy).then_inc(s_eh, 1)
                    if main and KINDS[q][u] != "N":
                        n = split_count(q, u)
                        act.wait_ge(s_z, at(i, per_u, UNITS * q + u + 1))
                        act.wait_ge(s_hmm, at(i, SPLITS, n - HR + 1))
                        v = unit_of_split(n - HR)
                        act.wait_ge(*low_done(i, v))
                        nc.scalar.activation(hr[:, n % HR, :], zr[:, (UNITS * q + u) % ZR, :],
                                             ACT.Copy).then_inc(s_h, 1)
                    if nxt and u == 1:
                        act.wait_ge(s_rep1, at(i, per_rep1, (C1 + 1) * q + 1))
                        act.wait_ge(s_z1, at(i, per_z1, C1 * q))
                        nc.scalar.activation(a1[:], ps[0:K1, BK_B1[0], :], ACT.Copy).then_inc(s_a1, 1)
                    if nxt and u == 8:
                        act.wait_ge(s_mm1, at(i, per_z1, C1 * (q + 1)))
                        act.wait_ge(s_a2[q % 2], at(i, 2 * 16 * G, 16 * G * ((q + 1) // 2)))
                        act.wait_ge(s_p1, at(i, TILES, q))
                        act.wait_ge(s_z, at(i, per_u, UNITS * q))
                        nc.scalar.activation(x1[:], ps[:, BK_ACC1, :], ACT.Relu, bias=b1_sb[:]).then_inc(s_x1, 1)
                    if nxt2 and u == 9:
                        act.wait_ge(s_tr, at(i, TILES, q + 1))
                        nc.scalar.activation(x0t[:, (q + 2) % TILES, :], ps[0:2 * M, BK_T, :],
                                             ACT.Copy).then_inc(s_x0t, 1)

                def tail(i, q):
                    act.wait_ge(s_unit, at(i, per_u, UNITS * (q + 1)))
                    act.wait_ge(s_p2, at(i, TILES, q))
                    nc.scalar.activation(x2[:], ps[:, BK_ACC2[q % 2], :], ACT.Relu, bias=b2_sb[:]).then_inc(s_x2, 1)

                run(act, step, tail, AHEAD_ACT)

                k = 0
                for layer, (src_bias, dst, groups) in enumerate(((bt1_sb, h1, F1 // P), (bt2_sb, h2, F2 // P))):
                    for c in range(groups):
                        for n in range(B // N):
                            k += 1
                            act.wait_ge(s_mlp, k)
                            nc.scalar.activation(dst[:, c, n * N:(n + 1) * N], ps[:, (k - 1) % 8, :], ACT.Relu,
                                                 bias=src_bias[:, c:c + 1]).then_inc(s_act, 1)
                for n in range(B // N):
                    k += 1
                    act.wait_ge(s_mlp, k)
                    nc.scalar.activation(y_sb[:, n * N:(n + 1) * N], ps[0:1, (k - 1) % 8, :],
                                         ACT.Copy).then_inc(s_act, 1)

            @block.vector
            def _(dve):
                credit(dve, [(s_el, 0), (s_z1, per_z1 - C1), (s_p1, TILES - 1), (s_z, per_u), (s_ld, DS),
                             (s_p2, TILES)])
                dve.wait_ge(s_w, 2)
                nc.vector.tensor_tensor(w2l[:], w2_stage, w2h[:], ALU.subtract).then_inc(s_wl, 1)
                nc.vector.tensor_tensor(w1_sb[:], w1_sb[:], w1b_stage, ALU.add).then_inc(s_wl, 1)
                dve.wait_ge(s_wl, 2)

                def step(i, q, u, main, nxt, nxt2):
                    if main:
                        j = u // 2
                        if u == 0:
                            par = q % 2
                            dve.wait_ge(s_a2[par], at(i, 2 * 16 * G, 16 * G * ((q + 1) // 2 if par else q // 2)))
                        dve.wait_ge(s_rep2, at(i, per_rep2, J * q + j - 1))
                        dve.wait_ge(*low_done(i, UNITS * q + u - ZR))
                        nc.vector.tensor_tensor(
                            zr[:, (UNITS * q + u) % ZR, :].rearrange("p (g n) -> p g n", n=N),
                            a2[:, q % 2, (u % 2) * UC:(u % 2 + 1) * UC, :],
                            ps[:, BK_B2[(J * q + j) % 2]:BK_B2[(J * q + j) % 2] + 1, :].to_broadcast([P, UC, N]),
                            ALU.mult).then_inc(s_z, 1)
                        if u and KINDS[q][u - 1] == "D":
                            n = split_count(q, u - 1)
                            dve.wait_ge(s_h, at(i, SPLITS, n + 1))
                            dve.wait_ge(s_unit, at(i, per_u, unit_of_split(n - LR) + 1))
                            nc.vector.tensor_tensor(lr[:, n % LR, :], zr[:, (UNITS * q + u - 1) % ZR, :],
                                                    hr[:, n % HR, :], ALU.subtract).then_inc(s_ld, 1)
                    if nxt2 and q == 2 and u == 3:
                        dve.wait_ge(s_eh, at(i, 1, 1))
                        nc.vector.tensor_tensor(e_hl[:, M:2 * M, :], e_raw[:], e_hl[:, 0:M, :],
                                                ALU.subtract).then_inc(s_el, 1)
                    if nxt:
                        for k in {3: (0, 1), 4: (2, 3), 5: (4, 5), 6: (6,)}.get(u, ()):
                            dve.wait_ge(s_rep1, at(i, per_rep1, (C1 + 1) * q + k + 2))
                            dve.wait_ge(s_a1, at(i, TILES, q + 1))
                            dve.wait_ge(s_mm1, at(i, per_z1, C1 * q + k - 1))
                            nc.vector.tensor_tensor(z1[:, (C1 * q + k) % 2, :], a1[:], ps[0:K1, BK_B1[(k + 1) % 2], :],
                                                    ALU.mult).then_inc(s_z1, 1)
                    if nxt and u == 9:
                        position_sum(i if q < TILES - 1 else i + 1, (q + 1) % TILES, x1, s_x1, at(i, TILES, q + 1),
                                     part1, p1, s_p1)

                def position_sum(i, q, x, ready, value, part, total, done):
                    dve.wait_ge(ready, value)
                    nc.vector.tensor_reduce(part[:, q, :], x[:].rearrange("s (d b) -> s b d", d=DT), AX_X,
                                            ALU.add).then_inc(done, 1)
                    if q == TILES - 1:
                        dve.wait_ge(done, at(i, TILES, TILES - 1) if done is s_p1 else at(i, TILES, TILES))
                        nc.vector.tensor_reduce(total[:, bass.ds(i * P, P)], part[:, :, :].rearrange("s q b -> s b q"),
                                                AX_X, ALU.add).then_inc(s_part, 1)

                def tail(i, q):
                    position_sum(i, q, x2, s_x2, at(i, TILES, q + 1), part2, p2, s_p2)

                run(dve, step, tail, AHEAD_DVE)

            @block.tensor
            def _(pe):
                credit(pe, [(s_tr, 2), (s_rep1, per_rep1 - C1 - 1), (s_mm1, per_z1 - C1), (s_rep2, per_rep2 - 2),
                            (s_hmm, SPLITS), (s_unit, per_u)])
                pe.wait_ge(s_w, 1)
                pe.wait_ge(s_const, 7 * 16)

                def rep2(i, q, j, extra):
                    jj = J * q + j
                    pe.wait_ge(s_z, at(i, per_u, UNITS * q + 2 * j - 2))
                    nc.tensor.matmul(ps[:, BK_B2[jj % 2], :], sel_r[:, j, :], x0t[:, q % TILES, :],
                                     start=True, stop=True).then_inc(s_rep2, 1)

                def rep1(i, q, e):
                    if e == 0:
                        pe.wait_ge(s_x0t, at(i, TILES, q))
                        pe.wait_ge(s_z1, at(i, per_z1, C1 * q - 1))
                    elif e == 2:
                        pe.wait_ge(s_a1, at(i, TILES, q + 1))
                    else:
                        pe.wait_ge(s_z1, at(i, per_z1, C1 * q + max(e - 2, 0)))
                    nc.tensor.matmul(ps[0:K1, BK_B1[e % 2], :], sel_r[:, J + e, 0:K1], x0t[:, (q + 1) % TILES, :],
                                     start=True, stop=True).then_inc(s_rep1, 1)

                def layer1(i, q, k):
                    if k == 0:
                        pe.wait_ge(s_x1, at(i, TILES, q))
                        pe.wait_ge(s_wl, 2)
                    pe.wait_ge(s_z1, at(i, per_z1, C1 * q + k + 1))
                    K = K1 if k < C1 - 1 else (SHIFTS - SC * (C1 - 1)) * M
                    nc.tensor.matmul(ps[:, BK_ACC1, :], w1_sb[0:K, k, :], z1[0:K, (C1 * q + k) % 2, :],
                                     start=(k == 0), stop=(k == C1 - 1)).then_inc(s_mm1, 1)

                def chunk(u, c):
                    return (u // 2) * G + (u % 2) * UC + c

                def high(i, q, u):
                    n = split_count(q, u)
                    if u == 0:
                        pe.wait_ge(s_x2, at(i, TILES, q - 1))
                    pe.wait_ge(s_h, at(i, SPLITS, n + 1))
                    for c in range(UC):
                        for w in (w2h, w2l):
                            mm = nc.tensor.matmul(ps[:, BK_ACC2[q % 2], :], w[:, chunk(u, c), :],
                                                  hr[:, n % HR, c * N:(c + 1) * N],
                                                  start=(u == 0 and c == 0 and w is w2h), stop=False)
                    mm.then_inc(s_hmm, 1)

                def finish(i, q, u):
                    last = u == UNITS - 1
                    if KINDS[q][u] == "N":
                        pe.wait_ge(s_z, at(i, per_u, UNITS * q + u + 1))
                        for c in range(UC):
                            mm = nc.tensor.matmul(ps[:, BK_ACC2[q % 2], :], w2n_sb[:, NATIVE.index(u), c, :],
                                                  zr[:, (UNITS * q + u) % ZR, c * N:(c + 1) * N],
                                                  start=False, stop=(last and c == UC - 1))
                    else:
                        pe.wait_ge(*low_done(i, UNITS * q + u))
                        n = split_count(q, u)
                        for c in range(UC):
                            mm = nc.tensor.matmul(ps[:, BK_ACC2[q % 2], :], w2h[:, chunk(u, c), :],
                                                  lr[:, n % LR, c * N:(c + 1) * N],
                                                  start=False, stop=(last and c == UC - 1))
                    mm.then_inc(s_unit, 1)

                def step(i, q, u, main, nxt, nxt2, before=True):
                    if main:
                        if u in (1, 3, 5):
                            rep2(i, q, (u + 3) // 2, 0)
                        if KINDS[q][u] != "N":
                            high(i, q, u)
                        if u >= LAG:
                            finish(i, q, u - LAG)
                        elif before and not (type(i) is int and i == 0 and q == 0):
                            finish(i - 1 if q == 0 else i, (q - 1) % TILES, u - LAG + UNITS)
                    if nxt:
                        for k in {3: (0, 1), 4: (2, 3), 5: (4, 5), 6: (6,)}.get(u, ()):
                            layer1(i, q, k)
                        for e in {0: (0, 1), 1: (2,), 2: (3, 4), 3: (5, 6), 4: (7,)}.get(u, ()):
                            rep1(i, q, e)
                        if u in (7, 9):
                            i1, q1 = (i, q + 1) if q < TILES - 1 else (i + 1, 0)
                            rep2(i1, q1, (u - 7) // 2, 0)
                    if nxt2 and u == 7:
                        if q == 2:
                            pe.wait_ge(s_el, at(i, 1, 1))
                        pe.wait_ge(s_x0t, at(i, TILES, q))
                        for d in range(DT):
                            mm = nc.tensor.transpose(ps[0:2 * M, BK_T, d * P:(d + 1) * P],
                                                     e_hl[:, :, DT * ((q + 2) % TILES) + d], ident_sb[:])
                        mm.then_inc(s_tr, 1)

                def tail(i, q):
                    if type(i) is int and i == BLOCKS - 1 and q == TILES - 1:
                        for u in range(UNITS - LAG, UNITS):
                            finish(i, q, u)

                run(pe, step, tail, AHEAD_PE)

                k = 0
                pe.wait_ge(s_mlpw, 4 * 16)
                pe.wait_ge(s_part, 2 * BLOCKS)
                pe.wait_ge(s_x2, at(BLOCKS - 1, TILES, TILES))
                for c in range(F1 // P):
                    for n in range(B // N):
                        cols, f = slice(n * N, (n + 1) * N), slice(c * P, (c + 1) * P)
                        nc.tensor.matmul(ps[:, k % 8, :], wt1_sb[:, 0, f], p1[:, cols], start=True, stop=False)
                        nc.tensor.matmul(ps[:, k % 8, :], wt1_sb[:, 1, f], p2[:, cols], start=False, stop=False)
                        nc.tensor.matmul(ps[:, k % 8, :], wt1c_sb[:, f], ctx_sb[:, cols], start=False,
                                         stop=True).then_inc(s_mlp, 1)
                        k += 1
                for c in range(F2 // P):
                    for n in range(B // N):
                        pe.wait_ge(s_act, 7 + n if c == 0 else 8)
                        for kk in range(F1 // P):
                            mm = nc.tensor.matmul(ps[:, k % 8, :], wt2_sb[:, kk, c * P:(c + 1) * P],
                                                  h1[:, kk, n * N:(n + 1) * N], start=(kk == 0),
                                                  stop=(kk == F1 // P - 1))
                        mm.then_inc(s_mlp, 1)
                        k += 1
                for n in range(B // N):
                    pe.wait_ge(s_act, 11 + n)
                    for kk in range(F2 // P):
                        mm = nc.tensor.matmul(ps[0:1, k % 8, :], wt3_sb[:, kk:kk + 1], h2[:, kk, n * N:(n + 1) * N],
                                              start=(kk == 0), stop=(kk == F2 // P - 1))
                    mm.then_inc(s_mlp, 1)
                    k += 1


def run(eng, step, tail, ahead):
    last = BLOCKS - 1

    def first_steps(i, q, nxt=True, nxt2=True):
        for u in range(ahead):
            step(i, q, u, True, nxt, nxt2)

    for u in range(UNITS):
        step(-1, TILES - 2, u, False, False, True)
    for u in range(UNITS):
        step(-1, TILES - 1, u, False, True, True)
    first_steps(0, 0)
    with eng.Fori(0, last) as i:
        for q in range(TILES):
            for u in range(ahead, UNITS):
                step(i, q, u, True, True, True)
            first_steps(i if q < TILES - 1 else i + 1, (q + 1) % TILES)
            tail(i, q)
    for q in range(TILES):
        for u in range(ahead, UNITS):
            step(last, q, u, True, q < TILES - 1, q < TILES - 2)
        if q < TILES - 1:
            first_steps(last, q + 1, q + 1 < TILES - 1, q + 1 < TILES - 2)
        tail(last, q)


def pair_rows():
    k, p = np.meshgrid(np.arange(C1), np.arange(K1), indexing="ij")
    shift, h = SC * k + p // M, p % M
    return h, (h + shift) % M, shift, shift < SHIFTS


def selection():
    sel = np.zeros((2 * M, SEL, P), np.float32)
    for j in range(J):
        for p in range(P):
            if MG * j + p % MG < M:
                sel[MG * j + p % MG, j, p] = 1
    h, m, _, there = pair_rows()
    for p in range(K1):
        sel[h[0, p], J, p] = 1
        for k in range(C1):
            if there[k, p]:
                sel[m[k, p], J + 1 + k, p] = 1
    sel[M:] = sel[:M]
    return sel


def kernel(**inputs):
    from concourse import bacc
    from concourse.bass_utils import run_bass_kernel_spmd

    x = {k: np.asarray(v) for k, v in inputs.items()}
    w1 = x["L0_rec_W1"]
    h, m, shift, there = pair_rows()
    w1a, w1b = np.zeros((2, K1, C1, S), w1.dtype)
    kk, pp = np.nonzero(there)
    w1a[pp, kk] = w1[:, h[kk, pp], m[kk, pp]].T
    kk, pp = np.nonzero(there & (shift > 0))
    w1b[pp, kk] = w1[:, m[kk, pp], h[kk, pp]].T
    w2 = np.zeros((HG, MG, J, G, S), x["L0_rec_W2"].dtype)
    by = x["L0_rec_W2"].transpose(1, 2, 0).reshape(G, HG, M, S)
    for j in range(J):
        mm = range(MG * j, min(MG * j + MG, M))
        w2[:, :len(mm), j] = by[:, :, mm.start:mm.stop].transpose(1, 2, 0, 3)
    w2 = w2.reshape(P, CHUNKS, S)
    arrays = {
        "ids": x["ids"],
        "w1a": w1a, "w1b": w1b, "b1": x["L0_rec_b1"].reshape(S, 1),
        "w2": w2, "w2n": w2.reshape(P, UNITS, UC, S)[:, NATIVE] if NATIVE else None,
        "b2": x["L0_rec_b2"].reshape(S, 1),
        "sel": selection(), "ident": np.eye(P, dtype=np.float32),
        "wt1": x["W_top1"][:2 * S].reshape(2, S, F1).transpose(1, 0, 2), "wt1c": x["W_top1"][2 * S:],
        "bt1": x["b_top1"].reshape(F1 // P, P).T,
        "wt2": x["W_top2"].reshape(F1 // P, P, F2).transpose(1, 0, 2),
        "bt2": x["b_top2"].reshape(F2 // P, P).T,
        "wt3": x["W_top3"].reshape(F2 // P, P).T,
        "ctx_t": x["dense_ctx"].T,
    }
    tables = {f"tbl_{f}": x[f"tbl_{f}"] for f in range(M)}
    nc = bacc.Bacc("TRN2", target_bir_lowering=False, num_devices=1)
    data, aps = {}, {}
    for name, a in {**arrays, **tables}.items():
        data[f"in_{name}"] = np.ascontiguousarray(a)
        aps[name] = nc.dram_tensor(f"in_{name}", a.shape, mybir.dt.from_np(a.dtype), kind="ExternalInput").ap()
    out = nc.dram_tensor("out_y", (B, 1), F32, kind="ExternalOutput").ap()
    cin_tower(nc, [aps[f"tbl_{f}"] for f in range(M)], **{k: aps[k] for k in arrays},
              out=out.rearrange("b o -> o b"))
    r = run_bass_kernel_spmd(nc, [data], core_ids=[0])
    return r.results[0]["out_y"]
```

```python
from contextlib import ExitStack

import numpy as np

import concourse.bass as bass
from concourse import mybir
from concourse.alu_op_type import AluOpType as ALU

ACT = mybir.ActivationFunctionType
F32 = mybir.dt.float32
F32R = mybir.dt.float32r
I32 = mybir.dt.int32
AX_X = mybir.AxisListType.X

P = 128
B, M, D = 1024, 39, 16
S = 128
CTX = 16
F1, F2 = 512, 256
BLOCKS = B // P
TILES = 4
DT = D // TILES
N = DT * P
MG, HG = 8, 16
J = -(-M // MG)
G = S // HG
CHUNKS = J * G
UC = 4
UNITS = CHUNKS // UC
SHIFTS = (M + 1) // 2
SC = 3
K1 = SC * M
C1 = -(-SHIFTS // SC)
SEL = J + C1

KINDS = ['PDPDPDPDDP', 'PDPDPDPDDP', 'PDPDPDPDDP', 'PDPDPDPDDP']
ZR, HR, LR = 4, 2, 4
REFILL = (8, 9)
NEXT_LOOKUPS = 2 * UNITS
LAG = 2
AHEAD_PE, AHEAD_ACT, AHEAD_DVE = 2, 4, 5

BK_B2, BK_ACC2, BK_ACC1, BK_B1, BK_T = (0, 1), (2, 3), 4, (5, 6), 7


def split_count(q, u):
    return sum(c != "N" for c in "".join(KINDS)[: UNITS * q + u])


LAP = "".join(KINDS)
SPLITS, PS, DS = (len(LAP) - LAP.count("N")), LAP.count("P"), LAP.count("D")
CONSTS = 6 + any(c == "N" for c in LAP)
NATIVE = sorted({u for k in KINDS for u, c in enumerate(k) if c == "N"})
assert SPLITS % HR == 0 and SPLITS % LR == 0 and len(LAP) % ZR == 0
assert all(k[0] != "N" and k[-1] != "D" for k in KINDS)


def at(i, per, k):
    return (i + 1) * per + k


def lookup_plan():
    steps = [w for w in range(len(LAP)) if LAP[w] != "P" and not UNITS + REFILL[0] <= w < NEXT_LOOKUPS]
    plan = [0] * len(LAP)
    for n, w in enumerate(steps):
        plan[w] = M * (n + 1) // len(steps) - M * n // len(steps)
    return plan


def ends_at(q, u):
    kinds = KINDS[(q - (u < 0)) % TILES]
    return u + 1 if kinds[u % UNITS] == "N" else u + LAG


def there(i, t):
    return not isinstance(i, int) or 0 <= TILES * i + t < TILES * BLOCKS


def layer1_phase(u):
    return (u - UNITS // 2, 2) if u >= UNITS // 2 else (u + UNITS // 2, 1)


def cin_tower(nc, tables, ids, w1a, w1b, b1, fold, w2, b2, sel, ident, wt1, wt1c, bt1, wt2, bt2, wt3, ctx_t, out, w2n=None):
    with ExitStack() as stack:
        def sb(name, shape, dt=F32):
            return stack.enter_context(nc.sbuf_tensor(name, shape, dt))

        def sem(name):
            return stack.enter_context(nc.semaphore(name))

        ps = stack.enter_context(nc.psum_tensor("ps", [P, 8, N], F32))

        ids_all = sb("ids_all", [P, BLOCKS, M], I32)
        ids_now = sb("ids_now", [P, M], I32)
        e_raw = sb("e_raw", [P, M, D])
        e_hl = sb("e_hl", [P, 2 * M, D])
        x0t = sb("x0t", [2 * M, TILES, N], F32R)
        sel_r = sb("sel_r", [2 * M, SEL, P], F32R)
        ident_sb = sb("ident_sb", [P, P])
        w1_sb = sb("w1_sb", [K1, C1, S])
        b1_sb = sb("b1_sb", [S, 1])
        b2_sb = sb("b2_sb", [S, 1])
        w2h = sb("w2h", [P, CHUNKS, S], F32R)
        w2l = sb("w2l", [P, CHUNKS, S], F32R)
        w2n_sb = sb("w2n_sb", [P, len(NATIVE), UC, S]) if NATIVE else None
        z1 = sb("z1", [K1, 2, N])
        x1 = sb("x1", [S, N])
        x2 = sb("x2", [S, N])
        a2 = sb("a2", [P, 2, G, N])
        zr = sb("zr", [P, ZR, UC * N])
        hr = sb("hr", [P, HR, UC * N], F32R)
        lr = sb("lr", [P, LR, UC * N], F32R)
        part1 = sb("part1", [S, TILES, P])
        part2 = sb("part2", [S, TILES, P])
        p1 = sb("p1", [S, B])
        p2 = sb("p2", [S, B])
        bt1_sb = sb("bt1_sb", [P, F1 // P])
        bt2_sb = sb("bt2_sb", [P, F2 // P])
        wt3_sb = sb("wt3_sb", [P, F2 // P])

        zflat = zr[:, :, :].rearrange("p a b -> p (a b)")
        aflat = a2[:, :, :, :].rearrange("p a b c -> p (a b c)")
        w2_stage = zflat[:, 0:CHUNKS * S].rearrange("p (c s) -> p c s", s=S)
        w1b_stage = zflat[0:K1, CHUNKS * S:(CHUNKS + C1) * S].rearrange("p (c s) -> p c s", s=S)
        fold_sb = zflat[0:K1, (CHUNKS + C1) * S:(CHUNKS + C1) * S + C1 * M].rearrange("p (c m) -> p c m", m=M)
        sel_stage = aflat[0:2 * M, 0:SEL * P].rearrange("p (c s) -> p c s", s=P)
        o = 0
        h1 = zflat[:, o:o + (F1 // P) * B].rearrange("p (c b) -> p c b", b=B)
        o += (F1 // P) * B
        wt1_sb = zflat[:, o:o + 2 * F1].rearrange("p (c f) -> p c f", f=F1)
        o += 2 * F1
        wt1c_sb = zflat[0:CTX, o:o + F1]
        o += F1
        ctx_sb = zflat[0:CTX, o:o + B]
        o += B
        wt2_sb = zflat[:, o:o + (F1 // P) * F2].rearrange("p (c f) -> p c f", f=F2)
        assert o + (F1 // P) * F2 <= ZR * UC * N
        h2 = aflat[:, 0:(F2 // P) * B].rearrange("p (c b) -> p c b", b=B)
        y_sb = aflat[0:1, (F2 // P) * B:(F2 // P) * B + B]

        s_ids = sem("s_ids")
        s_stage = sem("s_stage")
        s_const = sem("s_const")
        s_mlpw = sem("s_mlpw")
        s_now = sem("s_now")
        s_looked = sem("s_looked")
        s_eh = sem("s_eh")
        s_el = sem("s_el")
        s_tr = sem("s_tr")
        s_x0t = sem("s_x0t")
        s_rep1 = sem("s_rep1")
        s_z1 = sem("s_z1")
        s_mm1 = sem("s_mm1")
        s_x1 = sem("s_x1")
        s_a2 = [sem("s_a2_even"), sem("s_a2_odd")]
        s_p1 = sem("s_p1")
        s_rep2 = sem("s_rep2")
        s_z = sem("s_z")
        s_h = sem("s_h")
        s_lp = sem("s_lp")
        s_ld = sem("s_ld")
        s_hmm = sem("s_hmm")
        s_unit = sem("s_unit")
        s_x2 = sem("s_x2")
        s_p2 = sem("s_p2")
        s_w = sem("s_w")
        s_wl = sem("s_wl")
        s_fold = sem("s_fold")
        s_part = sem("s_part")
        s_mlp = sem("s_mlp")
        s_act = sem("s_act")
        s_out = sem("s_out")

        per_z1, per_rep1, per_rep2, per_u = TILES * C1, TILES * C1, TILES * J, TILES * UNITS

        def low_done(i, w):
            lap, w = divmod(w, per_u)
            if LAP[w] == "P":
                return s_lp, at(i, PS, LAP[:w].count("P") + 1 + lap * PS)
            if LAP[w] == "D":
                return s_ld, at(i, DS, LAP[:w].count("D") + 1 + lap * DS)
            return s_unit, at(i, per_u, w + 1 + lap * per_u)

        def unit_of_split(n):
            lap, n = divmod(n, SPLITS)
            return [k for k, c in enumerate(LAP) if c != "N"][n] + lap * per_u

        def credit(eng, pairs):
            for s, n in pairs:
                eng.sem_inc(s, n)

        with nc.Block() as block:
            @block.sync
            def _(sp):
                credit(sp, [(s_a2[0], 2 * 16 * G), (s_a2[1], 2 * 16 * G)])
                sp.dma_start(ids_all[:], ids.rearrange("(t p) m -> p t m", p=P)).then_inc(s_ids, 16)
                for dst, src in ((sel_stage, sel), (w2_stage, w2), (w1b_stage, w1b), (w1_sb[:], w1a), (fold_sb, fold)):
                    sp.dma_start(dst, src).then_inc(s_stage, 16)
                for dst, src in ((ident_sb[:], ident), (b1_sb[:], b1), (b2_sb[:], b2),
                                 (bt1_sb[:], bt1), (bt2_sb[:], bt2), (wt3_sb[:], wt3),
                                 *([(w2n_sb[:], w2n)] if NATIVE else [])):
                    sp.dma_start(dst, src).then_inc(s_const, 16)

                def replicate(i, t):
                    sp.wait_ge(s_x1, at(i, TILES, t + 1))
                    for g in range(G):
                        src = x1[g * HG:(g + 1) * HG, :].rearrange("p (o n) -> p o n", o=1)
                        sp.dma_start(a2[:, t % 2, g, :], src.to_broadcast([HG, MG, N])).then_inc(s_a2[t % 2], 16)

                replicate(-1, TILES)
                with sp.Fori(0, BLOCKS - 1) as i:
                    for q in range(TILES):
                        replicate(i, q + 1)
                for q in range(TILES - 1):
                    replicate(BLOCKS - 1, q + 1)
                sp.wait_ge(s_unit, at(BLOCKS - 1, per_u, per_u))
                sp.wait_ge(s_lp, at(BLOCKS - 1, PS, PS))
                for dst, src in ((wt1_sb, wt1), (wt1c_sb, wt1c), (ctx_sb, ctx_t), (wt2_sb, wt2)):
                    sp.dma_start(dst, src).then_inc(s_mlpw, 16)
                sp.wait_ge(s_act, (F1 // P + F2 // P + 1) * (B // N))
                sp.dma_start(out, y_sb).then_inc(s_out, 16)
                sp.wait_ge(s_out, 16)

            @block.gpsimd
            def _(pool):
                credit(pool, [(s_now, 1), (s_lp, PS)])

                def ids_of(i, block, k):
                    pool.wait_ge(s_looked, at(i, 16 * M, 16 * M * (block - 1)))
                    nc.gpsimd.tensor_copy(ids_now[:], ids_all[:, k, :]).then_inc(s_now, 1)
                    pool.wait_ge(s_now, at(i, 1, block + 1))
                    pool.wait_ge(s_el, at(i, 1, block))
                    pool.wait_ge(s_eh, at(i, 1, block))

                def look_up(m):
                    nc.gpsimd.indirect_dma_start(
                        e_raw[:, m, :], None, tables[m], bass.IndirectOffsetOnAxis(ids_now[:, m:m + 1], 0)
                    ).then_inc(s_looked, 16)

                def low(i, q, u):
                    n = split_count(q, u)
                    pool.wait_ge(s_h, at(i, SPLITS, n + 1))
                    pool.wait_ge(s_unit, at(i, per_u, unit_of_split(n - LR) + 1))
                    nc.gpsimd.tensor_tensor(lr[:, n % LR, :], zr[:, (UNITS * q + u) % ZR, :], hr[:, n % HR, :],
                                            ALU.subtract).then_inc(s_lp, 1)

                plan = lookup_plan()
                early = sum(plan[NEXT_LOOKUPS:])

                def lap(i, next_block=True, block_after=True):
                    for w in range(per_u):
                        if w == NEXT_LOOKUPS and block_after:
                            ids_of(i, 2, i + 2)
                        if LAP[w] == "P":
                            low(i, w // UNITS, w % UNITS)
                        if block_after if w >= NEXT_LOOKUPS else next_block:
                            first = sum(plan[NEXT_LOOKUPS:w]) if w >= NEXT_LOOKUPS else early + sum(plan[:w])
                            for m in range(first, first + plan[w]):
                                look_up(m)

                pool.wait_ge(s_ids, 16)
                ids_of(-1, 1, 0)
                for m in range(M):
                    look_up(m)
                ids_of(-1, 2, 1)
                for m in range(early):
                    look_up(m)
                with pool.Fori(0, BLOCKS - 2) as i:
                    lap(i)
                lap(BLOCKS - 2, block_after=False)
                lap(BLOCKS - 1, next_block=False, block_after=False)

            @block.scalar
            def _(act):
                credit(act, [(s_eh, 1), (s_x0t, TILES), (s_z1, per_z1), (s_x1, TILES), (s_h, SPLITS), (s_x2, TILES)])
                act.wait_ge(s_stage, 5 * 16)
                nc.scalar.activation(sel_r[:], sel_stage, ACT.Copy).then_inc(s_w, 1)
                nc.scalar.activation(w2h[:], w2_stage, ACT.Copy).then_inc(s_w, 1)
                act.wait_ge(s_const, CONSTS * 16)
                act.wait_ge(s_fold, 1)
                nc.scalar.activation(w1_sb[0:M, 0, :], ps[0:M, BK_ACC1, 0:S], ACT.Copy).then_inc(s_w, 1)

                def step(i, q, u):
                    if q == 1 and u == REFILL[0] and there(i, TILES):
                        act.wait_ge(s_looked, at(i, 16 * M, 16 * M))
                        act.wait_ge(s_tr, at(i, TILES, TILES))
                        nc.scalar.activation(e_hl[:, 0:M, :].bitcast(F32R), e_raw[:], ACT.Copy).then_inc(s_eh, 1)
                    if there(i, q) and KINDS[q][u] != "N":
                        n = split_count(q, u)
                        act.wait_ge(s_z, at(i, per_u, UNITS * q + u + 1))
                        act.wait_ge(s_hmm, at(i, SPLITS, n - HR + 1))
                        act.wait_ge(*low_done(i, unit_of_split(n - HR)))
                        nc.scalar.activation(hr[:, n % HR, :], zr[:, (UNITS * q + u) % ZR, :],
                                             ACT.Copy).then_inc(s_h, 1)
                    if u == 3 and there(i, q + 2):
                        act.wait_ge(s_tr, at(i, TILES, q + 3))
                        nc.scalar.activation(x0t[:, (q + 2) % TILES, :], ps[0:2 * M, BK_T, :],
                                             ACT.Copy).then_inc(s_x0t, 1)
                    v, ahead = layer1_phase(u)
                    t = q + ahead
                    k = C1 * t + v - 1
                    if 1 <= v <= C1 and there(i, t):
                        act.wait_ge(s_rep1, at(i, per_rep1, k + 1))
                        act.wait_ge(s_mm1, at(i, per_z1, k - 1))
                        nc.scalar.activation(z1[:, k % 2, :], ps[0:K1, BK_B1[k % 2], :], ACT.Square).then_inc(s_z1, 1)
                    if v == 9 and there(i, t):
                        act.wait_ge(s_mm1, at(i, per_z1, C1 * (t + 1)))
                        act.wait_ge(s_a2[(t - 1) % 2], at(i, 2 * 16 * G, 16 * G * ((t - 1) // 2 + 1)))
                        act.wait_ge(s_p1, at(i, TILES, t))
                        act.wait_ge(s_z, at(i, per_u, UNITS * (t - 1)))
                        nc.scalar.activation(x1[:], ps[:, BK_ACC1, :], ACT.Relu, bias=b1_sb[:],
                                             scale=0.5).then_inc(s_x1, 1)

                def tail(i, q):
                    act.wait_ge(s_unit, at(i, per_u, UNITS * (q + 1)))
                    act.wait_ge(s_p2, at(i, TILES, q))
                    nc.scalar.activation(x2[:], ps[:, BK_ACC2[q % 2], :], ACT.Relu, bias=b2_sb[:]).then_inc(s_x2, 1)

                run(act, step, tail, AHEAD_ACT)

                k = 0
                for layer, (src_bias, dst, groups) in enumerate(((bt1_sb, h1, F1 // P), (bt2_sb, h2, F2 // P))):
                    for c in range(groups):
                        for n in range(B // N):
                            k += 1
                            act.wait_ge(s_mlp, k)
                            nc.scalar.activation(dst[:, c, n * N:(n + 1) * N], ps[:, (k - 1) % 8, :], ACT.Relu,
                                                 bias=src_bias[:, c:c + 1]).then_inc(s_act, 1)
                for n in range(B // N):
                    k += 1
                    act.wait_ge(s_mlp, k)
                    nc.scalar.activation(y_sb[:, n * N:(n + 1) * N], ps[0:1, (k - 1) % 8, :],
                                         ACT.Copy).then_inc(s_act, 1)

            @block.vector
            def _(dve):
                credit(dve, [(s_el, 1), (s_p1, TILES), (s_z, per_u), (s_ld, DS), (s_p2, TILES)])
                dve.wait_ge(s_w, 2)
                nc.vector.tensor_tensor(w2l[:], w2_stage, w2h[:], ALU.subtract).then_inc(s_wl, 1)
                nc.vector.tensor_tensor(w1_sb[:], w1_sb[:], w1b_stage, ALU.add).then_inc(s_wl, 1)
                dve.wait_ge(s_wl, 2)

                def step(i, q, u):
                    if there(i, q):
                        j = u // 2
                        if u == 0:
                            dve.wait_ge(s_a2[q % 2], at(i, 2 * 16 * G, 16 * G * (q // 2 + 1)))
                        dve.wait_ge(s_rep2, at(i, per_rep2, J * q + j + 1))
                        dve.wait_ge(*low_done(i, UNITS * q + u - ZR))
                        bank = BK_B2[(J * q + j) % 2]
                        nc.vector.tensor_tensor(
                            zr[:, (UNITS * q + u) % ZR, :].rearrange("p (g n) -> p g n", n=N),
                            a2[:, q % 2, (u % 2) * UC:(u % 2 + 1) * UC, :],
                            ps[:, bank:bank + 1, :].to_broadcast([P, UC, N]), ALU.mult).then_inc(s_z, 1)
                        if u and KINDS[q][u - 1] == "D":
                            n = split_count(q, u - 1)
                            dve.wait_ge(s_h, at(i, SPLITS, n + 1))
                            dve.wait_ge(s_unit, at(i, per_u, unit_of_split(n - LR) + 1))
                            nc.vector.tensor_tensor(lr[:, n % LR, :], zr[:, (UNITS * q + u - 1) % ZR, :],
                                                    hr[:, n % HR, :], ALU.subtract).then_inc(s_ld, 1)
                    if q == 1 and u == REFILL[1] and there(i, TILES):
                        dve.wait_ge(s_eh, at(i, 1, 2))
                        nc.vector.tensor_tensor(e_hl[:, M:2 * M, :], e_raw[:], e_hl[:, 0:M, :],
                                                ALU.subtract).then_inc(s_el, 1)
                    if u == 6 and there(i, q + 1):
                        position_sum(i, q + 1, x1, s_x1, part1, p1, s_p1)

                def position_sum(i, t, x, ready, part, total, done):
                    dve.wait_ge(ready, at(i, TILES, t + 1))
                    nc.vector.tensor_reduce(part[:, t % TILES, :], x[:].rearrange("s (d b) -> s b d", d=DT), AX_X,
                                            ALU.add).then_inc(done, 1)
                    if t % TILES == TILES - 1:
                        dve.wait_ge(done, at(i, TILES, t + 1))
                        nc.vector.tensor_reduce(total[:, bass.ds(i * P, P)], part[:, :, :].rearrange("s q b -> s b q"),
                                                AX_X, ALU.add).then_inc(s_part, 1)

                def tail(i, q):
                    position_sum(i, q, x2, s_x2, part2, p2, s_p2)

                run(dve, step, tail, AHEAD_DVE)

            @block.tensor
            def _(pe):
                credit(pe, [(s_tr, TILES), (s_rep1, per_rep1), (s_mm1, per_z1), (s_rep2, per_rep2),
                            (s_hmm, SPLITS), (s_unit, per_u)])
                pe.wait_ge(s_w, 1)
                pe.wait_ge(s_const, CONSTS * 16)
                pe.wait_ge(s_wl, 2)
                for k in range(C1):
                    mm = nc.tensor.matmul(ps[0:M, BK_ACC1, 0:S], fold_sb[:, k, :], w1_sb[:, k, :], start=(k == 0),
                                          stop=(k == C1 - 1))
                mm.then_inc(s_fold, 1)

                def rep2(i, t, j):
                    jj = J * t + j
                    pe.wait_ge(s_z, at(i, per_u, UNITS * t + 2 * j - 2))
                    nc.tensor.matmul(ps[:, BK_B2[jj % 2], :], sel_r[:, j, :], x0t[:, t % TILES, :],
                                     start=True, stop=True).then_inc(s_rep2, 1)

                def rep1(i, t, k):
                    if k == 0:
                        pe.wait_ge(s_x0t, at(i, TILES, t + 1))
                    pe.wait_ge(s_z1, at(i, per_z1, C1 * t + k - 1))
                    nc.tensor.matmul(ps[0:K1, BK_B1[(C1 * t + k) % 2], :], sel_r[:, J + k, 0:K1],
                                     x0t[:, t % TILES, :], start=True, stop=True).then_inc(s_rep1, 1)

                def layer1(i, t, k):
                    if k == 0:
                        pe.wait_ge(s_x1, at(i, TILES, t))
                        pe.wait_ge(s_w, 3)
                    pe.wait_ge(s_z1, at(i, per_z1, C1 * t + k + 1))
                    K = K1 if k < C1 - 1 else (SHIFTS - SC * (C1 - 1)) * M
                    nc.tensor.matmul(ps[:, BK_ACC1, :], w1_sb[0:K, k, :], z1[0:K, (C1 * t + k) % 2, :],
                                     start=(k == 0), stop=(k == C1 - 1)).then_inc(s_mm1, 1)

                def chunk(u, c):
                    return (u // 2) * G + (u % 2) * UC + c

                def high(i, q, u):
                    n = split_count(q, u)
                    if u == 0:
                        pe.wait_ge(s_x2, at(i, TILES, q - 1))
                    pe.wait_ge(s_h, at(i, SPLITS, n + 1))
                    for c in range(UC):
                        for w in (w2h, w2l):
                            mm = nc.tensor.matmul(ps[:, BK_ACC2[q % 2], :], w[:, chunk(u, c), :],
                                                  hr[:, n % HR, c * N:(c + 1) * N],
                                                  start=(u == 0 and c == 0 and w is w2h), stop=False)
                    mm.then_inc(s_hmm, 1)

                def finish(i, q, u):
                    last = u == UNITS - 1
                    if KINDS[q][u] == "N":
                        pe.wait_ge(s_z, at(i, per_u, UNITS * q + u + 1))
                        for c in range(UC):
                            mm = nc.tensor.matmul(ps[:, BK_ACC2[q % 2], :], w2n_sb[:, NATIVE.index(u), c, :],
                                                  zr[:, (UNITS * q + u) % ZR, c * N:(c + 1) * N],
                                                  start=False, stop=(last and c == UC - 1))
                    else:
                        pe.wait_ge(*low_done(i, UNITS * q + u))
                        n = split_count(q, u)
                        for c in range(UC):
                            mm = nc.tensor.matmul(ps[:, BK_ACC2[q % 2], :], w2h[:, chunk(u, c), :],
                                                  lr[:, n % LR, c * N:(c + 1) * N],
                                                  start=False, stop=(last and c == UC - 1))
                    mm.then_inc(s_unit, 1)

                def step(i, q, u):
                    if there(i, q):
                        if u in (1, 3, 5):
                            rep2(i, q, (u + 3) // 2)
                        if KINDS[q][u] != "N":
                            high(i, q, u)
                    for w in range(u - LAG, u):
                        if ends_at(q, w) == u:
                            before = w < 0
                            if there(i, q - before):
                                finish(i - 1 if before and q == 0 else i, (q - before) % TILES, w % UNITS)
                    v, ahead = layer1_phase(u)
                    t = q + ahead
                    if there(i, t):
                        if v < C1:
                            rep1(i, t, v)
                        if 1 <= v <= C1:
                            layer1(i, t, v - 1)
                    if u in (7, 9) and there(i, q + 1):
                        rep2(i, q + 1, (u - 7) // 2)
                    if u == 1 and there(i, q + 2):
                        if q == 2:
                            pe.wait_ge(s_el, at(i, 1, 2))
                        pe.wait_ge(s_x0t, at(i, TILES, q + 2))
                        for d in range(DT):
                            mm = nc.tensor.transpose(ps[0:2 * M, BK_T, d * P:(d + 1) * P],
                                                     e_hl[:, :, DT * ((q + 2) % TILES) + d], ident_sb[:])
                        mm.then_inc(s_tr, 1)

                def tail(i, q):
                    if not there(i, q + 1):
                        for u in range(UNITS - LAG, UNITS):
                            if ends_at(q, u) >= UNITS:
                                finish(i, q, u)

                run(pe, step, tail, AHEAD_PE)

                k = 0
                pe.wait_ge(s_mlpw, 4 * 16)
                pe.wait_ge(s_part, 2 * BLOCKS)
                pe.wait_ge(s_x2, at(BLOCKS - 1, TILES, TILES))
                for c in range(F1 // P):
                    for n in range(B // N):
                        cols, f = slice(n * N, (n + 1) * N), slice(c * P, (c + 1) * P)
                        nc.tensor.matmul(ps[:, k % 8, :], wt1_sb[:, 0, f], p1[:, cols], start=True, stop=False)
                        nc.tensor.matmul(ps[:, k % 8, :], wt1_sb[:, 1, f], p2[:, cols], start=False, stop=False)
                        nc.tensor.matmul(ps[:, k % 8, :], wt1c_sb[:, f], ctx_sb[:, cols], start=False,
                                         stop=True).then_inc(s_mlp, 1)
                        k += 1
                for c in range(F2 // P):
                    for n in range(B // N):
                        pe.wait_ge(s_act, (F1 // P - 1) * (B // N) + n + 1)
                        for kk in range(F1 // P):
                            mm = nc.tensor.matmul(ps[:, k % 8, :], wt2_sb[:, kk, c * P:(c + 1) * P],
                                                  h1[:, kk, n * N:(n + 1) * N], start=(kk == 0),
                                                  stop=(kk == F1 // P - 1))
                        mm.then_inc(s_mlp, 1)
                        k += 1
                for n in range(B // N):
                    pe.wait_ge(s_act, (F1 // P + F2 // P - 1) * (B // N) + n + 1)
                    for kk in range(F2 // P):
                        mm = nc.tensor.matmul(ps[0:1, k % 8, :], wt3_sb[:, kk:kk + 1], h2[:, kk, n * N:(n + 1) * N],
                                              start=(kk == 0), stop=(kk == F2 // P - 1))
                    mm.then_inc(s_mlp, 1)
                    k += 1


def run(eng, step, tail, ahead):
    last = BLOCKS - 1

    def rest(i, q):
        for u in range(ahead, UNITS):
            step(i, q, u)
        if there(i, q + 1):
            for u in range(ahead):
                step(i if q < TILES - 1 else i + 1, (q + 1) % TILES, u)
        tail(i, q)

    for q in range(1, TILES):
        for u in range(UNITS):
            step(-1, q, u)
    for u in range(ahead):
        step(0, 0, u)
    with eng.Fori(0, last) as i:
        for q in range(TILES):
            rest(i, q)
    for q in range(TILES):
        rest(last, q)


def pair_rows():
    k, p = np.meshgrid(np.arange(C1), np.arange(K1), indexing="ij")
    shift, h = SC * k + p // M, p % M
    return h, (h + shift) % M, shift, shift < SHIFTS


def selection():
    sel = np.zeros((2 * M, SEL, P), np.float32)
    for j in range(J):
        for p in range(P):
            if MG * j + p % MG < M:
                sel[MG * j + p % MG, j, p] = 1
    h, m, _, there = pair_rows()
    for p in range(K1):
        for k in range(C1):
            if there[k, p]:
                sel[[h[k, p], m[k, p]], J + k, p] = 1
    sel[M:] = sel[:M]
    return sel


def kernel(**inputs):
    from concourse import bacc
    from concourse.bass_utils import run_bass_kernel_spmd

    x = {k: np.asarray(v) for k, v in inputs.items()}
    w1 = x["L0_rec_W1"]
    h, m, shift, there = pair_rows()
    w1a, w1b = np.zeros((2, K1, C1, S), w1.dtype)
    kk, pp = np.nonzero(there)
    w1a[pp, kk] = w1[:, h[kk, pp], m[kk, pp]].T
    w1b[pp, kk] = w1[:, m[kk, pp], h[kk, pp]].T
    fold = np.zeros((K1, C1, M), np.float32)
    kk, pp = np.nonzero(there)
    for row in (h, m):
        fold[pp, kk, row[kk, pp]] = np.where(shift[kk, pp] > 0, -1, 1)
    w2 = np.zeros((HG, MG, J, G, S), x["L0_rec_W2"].dtype)
    by = x["L0_rec_W2"].transpose(1, 2, 0).reshape(G, HG, M, S)
    for j in range(J):
        mm = range(MG * j, min(MG * j + MG, M))
        w2[:, :len(mm), j] = by[:, :, mm.start:mm.stop].transpose(1, 2, 0, 3)
    w2 = w2.reshape(P, CHUNKS, S)
    arrays = {
        "ids": x["ids"],
        "w1a": w1a, "w1b": w1b, "b1": x["L0_rec_b1"].reshape(S, 1), "fold": fold,
        "w2": w2,
        "b2": x["L0_rec_b2"].reshape(S, 1),
        "sel": selection(), "ident": np.eye(P, dtype=np.float32),
        "wt1": x["W_top1"][:2 * S].reshape(2, S, F1).transpose(1, 0, 2), "wt1c": x["W_top1"][2 * S:],
        "bt1": x["b_top1"].reshape(F1 // P, P).T,
        "wt2": x["W_top2"].reshape(F1 // P, P, F2).transpose(1, 0, 2),
        "bt2": x["b_top2"].reshape(F2 // P, P).T,
        "wt3": x["W_top3"].reshape(F2 // P, P).T,
        "ctx_t": x["dense_ctx"].T,
    }
    if NATIVE:
        arrays["w2n"] = w2.reshape(P, UNITS, UC, S)[:, NATIVE]
    tables = {f"tbl_{f}": x[f"tbl_{f}"] for f in range(M)}
    nc = bacc.Bacc("TRN2", target_bir_lowering=False, num_devices=1)
    data, aps = {}, {}
    for name, a in {**arrays, **tables}.items():
        data[f"in_{name}"] = np.ascontiguousarray(a)
        aps[name] = nc.dram_tensor(f"in_{name}", a.shape, mybir.dt.from_np(a.dtype), kind="ExternalInput").ap()
    out = nc.dram_tensor("out_y", (B, 1), F32, kind="ExternalOutput").ap()
    cin_tower(nc, [aps[f"tbl_{f}"] for f in range(M)], **{k: aps[k] for k in arrays},
              out=out.rearrange("b o -> o b"))
    r = run_bass_kernel_spmd(nc, [data], core_ids=[0])
    return r.results[0]["out_y"]
```

```python
from contextlib import ExitStack

import numpy as np

import concourse.bass as bass
from concourse import mybir
from concourse.alu_op_type import AluOpType as ALU

ACT = mybir.ActivationFunctionType
F32 = mybir.dt.float32
F32R = mybir.dt.float32r
I32 = mybir.dt.int32
AX_X = mybir.AxisListType.X

P = 128
B, M, D = 1024, 39, 16
S = 128
CTX = 16
F1, F2 = 512, 256
BLOCKS = B // P
TILES = 4
DT = D // TILES
N = DT * P
MG, HG = 8, 16
J = -(-M // MG)
G = S // HG
CHUNKS = J * G
UC = 4
UNITS = CHUNKS // UC
SHIFTS = (M + 1) // 2
SC = 3
K1 = SC * M
C1 = -(-SHIFTS // SC)
SEL = J + C1

KINDS = ["PDPDPDPDDP", "DDPPDPDPDP", "PDPDPPDDPP", "PDPDPDPDDP"]
ZR, HR, LR = 4, 2, 4
REFILL = (8, 9)
NEXT_LOOKUPS = 2 * UNITS
TRANSPOSE_STEP, X0T_STEP = 1, 3
LAG = 2
AHEAD_PE, AHEAD_ACT, AHEAD_DVE = 2, 4, 6

BK_B2, BK_ACC2, BK_ACC1, BK_B1, BK_T = (0, 1), (2, 3), 4, (5, 6), 7

HALVES = B // N
MLP = ([(1, 0, c) for c in range(F1 // P)] + [(2, 0, c) for c in range(F2 // P)] + [(1, 1, c) for c in range(F1 // P)]
       + [(3, 0, 0)] + [(2, 1, c) for c in range(F2 // P)] + [(3, 1, 0)])
MLP1_FIRST = (5, 6, 7, 8)
MLP1_START = (2, 4, 6, 8)
assert HALVES == 2

LAP = "".join(KINDS)
PS, DS = LAP.count("P"), LAP.count("D")
assert all(len(LAP) % slots == 0 for slots in (ZR, HR, LR))
assert all(k[-1] != "D" for k in KINDS)


def at(i, per, k):
    return (i + 1) * per + k


def lookup_plan():
    steps = [w for w in range(len(LAP)) if LAP[w] != "P" and not UNITS + REFILL[0] <= w < NEXT_LOOKUPS]
    plan = [0] * len(LAP)
    for n, w in enumerate(steps):
        plan[w] = M * (n + 1) // len(steps) - M * n // len(steps)
    return plan


def there(i, t):
    return not isinstance(i, int) or 0 <= TILES * i + t < TILES * BLOCKS


def last_lap(i):
    return isinstance(i, int) and i == BLOCKS - 1


def mlp_bank(layer, n, c):
    if layer == 1:
        return (BK_ACC1, *BK_B1, BK_T)[c]
    if layer == 2:
        return (BK_ACC2[0], BK_B2[0])[c]
    return (BK_B2[1], BK_ACC2[1])[n]


def layer1_phase(u):
    return (u - UNITS // 2, 2) if u >= UNITS // 2 else (u + UNITS // 2, 1)


def cin_tower(nc, tables, ids, w1a, w1b, b1, fold, w2, b2, sel, ident, wt1, wt1c, bt1, wt2, bt2, wt3, ctx_t, out):
    with ExitStack() as stack:
        def sb(name, shape, dt=F32):
            return stack.enter_context(nc.sbuf_tensor(name, shape, dt))

        def sem(name):
            return stack.enter_context(nc.semaphore(name))

        ps = stack.enter_context(nc.psum_tensor("ps", [P, 8, N], F32))

        ids_all = sb("ids_all", [P, BLOCKS, M], I32)
        ids_now = sb("ids_now", [P, M], I32)
        rows = sb("rows", [P, 3 * M * D])
        e_raw = rows[:, 0:M * D].rearrange("p (m d) -> p m d", d=D)
        e_hl = rows[:, M * D:3 * M * D].rearrange("p (m d) -> p m d", d=D)
        x0t = sb("x0t", [2 * M, TILES, N], F32R)
        sel_r = sb("sel_r", [2 * M, SEL, P], F32R)
        ident_sb = sb("ident_sb", [P, P])
        w1_sb = sb("w1_sb", [K1, C1, S])
        b1_sb = sb("b1_sb", [S, 1])
        b2_sb = sb("b2_sb", [S, 1])
        w2h = sb("w2h", [P, CHUNKS, S], F32R)
        w2l = sb("w2l", [P, CHUNKS, S], F32R)
        z1 = sb("z1", [P, 2, N])
        x1 = sb("x1", [S, N])
        x2 = sb("x2", [S, N])
        a2 = sb("a2", [P, 2, G, N])
        zr = sb("zr", [P, ZR, UC * N])
        hr = sb("hr", [P, HR, UC * N], F32R)
        lr = sb("lr", [P, LR, UC * N], F32R)
        part1 = sb("part1", [S, TILES, P])
        part2 = sb("part2", [S, TILES, P])
        p1 = sb("p1", [S, B])
        p2 = sb("p2", [S, B])
        bt1_sb = sb("bt1_sb", [P, F1 // P])
        bt2_sb = sb("bt2_sb", [P, F2 // P])
        wt2_sb = sb("wt2_sb", [P, F1 // P, F2])
        ctx_sb = sb("ctx_sb", [CTX, B])
        wt3_sb = sb("wt3_sb", [P, F2 // P])

        zflat = zr[:, :, :].rearrange("p a b -> p (a b)")
        aflat = a2[:, :, :, :].rearrange("p a b c -> p (a b c)")
        w2_stage = zflat[:, 0:CHUNKS * S].rearrange("p (c s) -> p c s", s=S)
        w1b_stage = zflat[0:K1, CHUNKS * S:(CHUNKS + C1) * S].rearrange("p (c s) -> p c s", s=S)
        fold_sb = zflat[0:K1, (CHUNKS + C1) * S:(CHUNKS + C1) * S + C1 * M].rearrange("p (c m) -> p c m", m=M)
        sel_stage = aflat[0:2 * M, 0:SEL * P].rearrange("p (c s) -> p c s", s=P)
        wt1_sb = rows[:, 0:2 * F1].rearrange("p (c f) -> p c f", f=F1)
        wt1c_sb = rows[0:CTX, 2 * F1:3 * F1]

        def hidden(layer, n, c):
            if layer == 1:
                return a2[:, 0, n * (F1 // P) + c, :]
            if layer == 2:
                return z1[:, c, :] if n == 0 else a2[:, 1, c, :]
            return a2[0:1, 1, F2 // P + n, :]

        s_ids_first = sem("s_ids_first")
        s_ids = sem("s_ids")
        s_stage = sem("s_stage")
        s_const = sem("s_const")
        s_mlpw = sem("s_mlpw")
        s_now = sem("s_now")
        s_looked = sem("s_looked")
        s_eh = sem("s_eh")
        s_el = sem("s_el")
        s_tr = sem("s_tr")
        s_x0t = sem("s_x0t")
        s_rep1 = sem("s_rep1")
        s_z1 = sem("s_z1")
        s_mm1 = sem("s_mm1")
        s_x1 = sem("s_x1")
        s_a2 = [[sem(f"s_a2_{tile}_{g}") for g in ("low_g", "high_g")] for tile in ("even", "odd")]
        s_p1 = sem("s_p1")
        s_rep2 = sem("s_rep2")
        s_z = sem("s_z")
        s_h = sem("s_h")
        s_lp = sem("s_lp")
        s_ld = sem("s_ld")
        s_hmm = sem("s_hmm")
        s_unit = sem("s_unit")
        s_x2 = sem("s_x2")
        s_p2 = sem("s_p2")
        s_w = sem("s_w")
        s_wl = sem("s_wl")
        s_fold = sem("s_fold")
        s_part = sem("s_part")
        s_mlp = sem("s_mlp")
        s_act = sem("s_act")
        s_out = sem("s_out")

        per_z1, per_rep1, per_rep2, per_u = TILES * C1, TILES * C1, TILES * J, TILES * UNITS

        constants = ((ident_sb[:], ident), (b1_sb[:], b1), (b2_sb[:], b2), (bt1_sb[:], bt1), (bt2_sb[:], bt2),
                     (wt3_sb[:], wt3), (wt2_sb[:], wt2), (ctx_sb[:], ctx_t))

        def low_done(i, w):
            lap, w = divmod(w, per_u)
            if LAP[w] == "P":
                return s_lp, at(i, PS, LAP[:w].count("P") + 1 + lap * PS)
            return s_ld, at(i, DS, LAP[:w].count("D") + 1 + lap * DS)

        def credit(eng, pairs):
            for s, n in pairs:
                eng.sem_inc(s, n)

        with nc.Block() as block:
            @block.sync
            def _(sp):
                credit(sp, [(s, 2 * 16 * UC) for both in s_a2 for s in both])
                sp.dma_start(ids_now[:], ids[0:P, :]).then_inc(s_ids_first, 16)
                sp.dma_start(ids_all[:], ids.rearrange("(t p) m -> p t m", p=P)).then_inc(s_ids, 16)
                for dst, src in ((sel_stage, sel), (w2_stage, w2), (w1b_stage, w1b), (w1_sb[:], w1a), (fold_sb, fold)):
                    sp.dma_start(dst, src).then_inc(s_stage, 16)
                for dst, src in constants:
                    sp.dma_start(dst, src).then_inc(s_const, 16)

                def replicate(i, t):
                    sp.wait_ge(s_x1, at(i, TILES, t + 1))
                    for g in range(G):
                        src = x1[g * HG:(g + 1) * HG, :].rearrange("p (o n) -> p o n", o=1)
                        sp.dma_start(a2[:, t % 2, g, :],
                                     src.to_broadcast([HG, MG, N])).then_inc(s_a2[t % 2][g // UC], 16)

                replicate(-1, TILES)
                with sp.Fori(0, BLOCKS - 1) as i:
                    for q in range(TILES):
                        replicate(i, q + 1)
                for q in range(TILES - 2):
                    replicate(BLOCKS - 1, q + 1)
                sp.wait_ge(s_tr, at(BLOCKS - 1, TILES, TILES))
                for dst, src in ((wt1_sb, wt1), (wt1c_sb, wt1c)):
                    sp.dma_start(dst, src).then_inc(s_mlpw, 16)
                replicate(BLOCKS - 1, TILES - 1)
                sp.wait_ge(s_act, len(MLP))
                y = a2[0:1, 1, F2 // P:F2 // P + HALVES, :].rearrange("p n b -> p (n b)")
                sp.dma_start(out, y).then_inc(s_out, 16)
                sp.wait_ge(s_out, 16)

            @block.gpsimd
            def _(pool):
                credit(pool, [(s_now, 2), (s_lp, PS)])

                def ids_of(i, block, k):
                    pool.wait_ge(s_looked, at(i, 16 * M, 16 * M * (block - 1)))
                    nc.gpsimd.tensor_copy(ids_now[:], ids_all[:, k, :]).then_inc(s_now, 1)
                    pool.wait_ge(s_now, at(i, 1, block + 1))
                    pool.wait_ge(s_el, at(i, 1, block))
                    pool.wait_ge(s_eh, at(i, 1, block))

                def look_up(m):
                    nc.gpsimd.indirect_dma_start(
                        e_raw[:, m, :], None, tables[m], bass.IndirectOffsetOnAxis(ids_now[:, m:m + 1], 0)
                    ).then_inc(s_looked, 16)

                def low(i, q, u):
                    w = UNITS * q + u
                    pool.wait_ge(s_h, at(i, per_u, w + 1))
                    pool.wait_ge(s_unit, at(i, per_u, w - LR + 1))
                    nc.gpsimd.tensor_tensor(lr[:, w % LR, :], zr[:, w % ZR, :], hr[:, w % HR, :],
                                            ALU.subtract).then_inc(s_lp, 1)

                plan = lookup_plan()
                early = sum(plan[NEXT_LOOKUPS:])

                def lap(i, next_block=True, block_after=True):
                    for w in range(per_u):
                        if w == NEXT_LOOKUPS and block_after:
                            ids_of(i, 2, i + 2)
                        if LAP[w] == "P":
                            low(i, w // UNITS, w % UNITS)
                        if block_after if w >= NEXT_LOOKUPS else next_block:
                            first = sum(plan[NEXT_LOOKUPS:w]) if w >= NEXT_LOOKUPS else early + sum(plan[:w])
                            for m in range(first, first + plan[w]):
                                look_up(m)

                pool.wait_ge(s_ids_first, 16)
                for m in range(M):
                    look_up(m)
                pool.wait_ge(s_ids, 16)
                ids_of(-1, 2, 1)
                for m in range(early):
                    look_up(m)
                with pool.Fori(0, BLOCKS - 2) as i:
                    lap(i)
                lap(BLOCKS - 2, block_after=False)
                lap(BLOCKS - 1, next_block=False, block_after=False)

            @block.scalar
            def _(act):
                credit(act, [(s_eh, 1), (s_x0t, TILES), (s_z1, per_z1), (s_x1, TILES), (s_h, per_u), (s_x2, TILES)])
                act.wait_ge(s_stage, 5 * 16)
                nc.scalar.activation(sel_r[:], sel_stage, ACT.Copy).then_inc(s_w, 1)
                nc.scalar.activation(w2h[:], w2_stage, ACT.Copy).then_inc(s_w, 1)
                act.wait_ge(s_const, 16 * len(constants))
                act.wait_ge(s_fold, 1)
                nc.scalar.activation(w1_sb[0:M, 0, :], ps[0:M, BK_ACC1, 0:S], ACT.Copy).then_inc(s_w, 1)

                def mlp(k):
                    layer, n, c = MLP[k]
                    if layer == 1 and n == 0:
                        act.wait_ge(s_z, at(BLOCKS - 1, per_u, UNITS * 3))
                    if layer == 2 and n == 0:
                        act.wait_ge(s_mm1, at(BLOCKS - 1, per_z1, per_z1))
                    if layer == 2 and n == 1:
                        act.wait_ge(s_z, at(BLOCKS - 1, per_u, per_u))
                    act.wait_ge(s_mlp, k + 1)
                    if layer == 3:
                        nc.scalar.activation(hidden(*MLP[k]), ps[0:1, mlp_bank(*MLP[k]), :], ACT.Copy).then_inc(s_act, 1)
                    else:
                        bias = (bt1_sb if layer == 1 else bt2_sb)[:, c:c + 1]
                        nc.scalar.activation(hidden(*MLP[k]), ps[:, mlp_bank(*MLP[k]), :], ACT.Relu,
                                             bias=bias).then_inc(s_act, 1)

                def step(i, q, u):
                    if q == 1 and u == REFILL[0] and there(i, TILES):
                        act.wait_ge(s_looked, at(i, 16 * M, 16 * M))
                        act.wait_ge(s_tr, at(i, TILES, TILES))
                        nc.scalar.activation(e_hl[:, 0:M, :].bitcast(F32R), e_raw[:], ACT.Copy).then_inc(s_eh, 1)
                    if there(i, q):
                        w = UNITS * q + u
                        act.wait_ge(s_z, at(i, per_u, w + 1))
                        act.wait_ge(s_hmm, at(i, per_u, w - HR + 1))
                        act.wait_ge(*low_done(i, w - HR))
                        nc.scalar.activation(hr[:, w % HR, :], zr[:, w % ZR, :], ACT.Copy).then_inc(s_h, 1)
                    if u == X0T_STEP and there(i, q + 2):
                        act.wait_ge(s_tr, at(i, TILES, q + 3))
                        nc.scalar.activation(x0t[:, (q + 2) % TILES, :], ps[0:2 * M, BK_T, :],
                                             ACT.Copy).then_inc(s_x0t, 1)
                    v, ahead = layer1_phase(u)
                    t = q + ahead
                    k = C1 * t + v - 1
                    if 1 <= v <= C1 and there(i, t):
                        act.wait_ge(s_rep1, at(i, per_rep1, k + 1))
                        act.wait_ge(s_mm1, at(i, per_z1, k - 1))
                        nc.scalar.activation(z1[0:K1, k % 2, :], ps[0:K1, BK_B1[k % 2], :], ACT.Square).then_inc(s_z1, 1)
                    if v == 9 and there(i, t):
                        act.wait_ge(s_mm1, at(i, per_z1, C1 * (t + 1)))
                        for half in range(2):
                            act.wait_ge(s_a2[(t - 1) % 2][half], at(i, 2 * 16 * UC, 16 * UC * ((t - 1) // 2 + 1)))
                        act.wait_ge(s_p1, at(i, TILES, t))
                        act.wait_ge(s_z, at(i, per_u, UNITS * (t - 1)))
                        nc.scalar.activation(x1[:], ps[:, BK_ACC1, :], ACT.Relu, bias=b1_sb[:],
                                             scale=0.5).then_inc(s_x1, 1)

                    if last_lap(i) and q == 3 and u < F1 // P:
                        mlp(u)

                def tail(i, q):
                    if last_lap(i) and q == 3:
                        mlp(F1 // P)
                    act.wait_ge(s_unit, at(i, per_u, UNITS * (q + 1)))
                    act.wait_ge(s_p2, at(i, TILES, q))
                    nc.scalar.activation(x2[:], ps[:, BK_ACC2[q % 2], :], ACT.Relu, bias=b2_sb[:]).then_inc(s_x2, 1)

                run(act, step, tail, AHEAD_ACT)

                for k in range(F1 // P + 1, len(MLP)):
                    mlp(k)

            @block.vector
            def _(dve):
                credit(dve, [(s_el, 1), (s_p1, TILES), (s_z, per_u), (s_ld, DS), (s_p2, TILES)])
                dve.wait_ge(s_w, 2)
                nc.vector.tensor_tensor(w2l[:], w2_stage, w2h[:], ALU.subtract).then_inc(s_wl, 1)
                nc.vector.tensor_tensor(w1_sb[:], w1_sb[:], w1b_stage, ALU.add).then_inc(s_wl, 1)
                dve.wait_ge(s_wl, 2)

                def step(i, q, u):
                    if there(i, q):
                        j = u // 2
                        if u < 2:
                            dve.wait_ge(s_a2[q % 2][u], at(i, 2 * 16 * UC, 16 * UC * (q // 2 + 1)))
                        dve.wait_ge(s_rep2, at(i, per_rep2, J * q + j + 1))
                        dve.wait_ge(*low_done(i, UNITS * q + u - ZR))
                        bank = BK_B2[(J * q + j) % 2]
                        nc.vector.tensor_tensor(
                            zr[:, (UNITS * q + u) % ZR, :].rearrange("p (g n) -> p g n", n=N),
                            a2[:, q % 2, (u % 2) * UC:(u % 2 + 1) * UC, :],
                            ps[:, bank:bank + 1, :].to_broadcast([P, UC, N]), ALU.mult).then_inc(s_z, 1)
                        if u and KINDS[q][u - 1] == "D":
                            w = UNITS * q + u - 1
                            dve.wait_ge(s_h, at(i, per_u, w + 1))
                            dve.wait_ge(s_unit, at(i, per_u, w - LR + 1))
                            nc.vector.tensor_tensor(lr[:, w % LR, :], zr[:, w % ZR, :], hr[:, w % HR, :],
                                                    ALU.subtract).then_inc(s_ld, 1)
                    if q == 1 and u == REFILL[1] and there(i, TILES):
                        dve.wait_ge(s_eh, at(i, 1, 2))
                        nc.vector.tensor_tensor(e_hl[:, M:2 * M, :], e_raw[:], e_hl[:, 0:M, :],
                                                ALU.subtract).then_inc(s_el, 1)
                    if u == 6 and there(i, q + 1):
                        position_sum(i, q + 1, x1, s_x1, part1, p1, s_p1)

                def position_sum(i, t, x, ready, part, total, done):
                    dve.wait_ge(ready, at(i, TILES, t + 1))
                    nc.vector.tensor_reduce(part[:, t % TILES, :], x[:].rearrange("s (d b) -> s b d", d=DT), AX_X,
                                            ALU.add).then_inc(done, 1)
                    if t % TILES == TILES - 1:
                        dve.wait_ge(done, at(i, TILES, t + 1))
                        nc.vector.tensor_reduce(total[:, bass.ds(i * P, P)], part[:, :, :].rearrange("s q b -> s b q"),
                                                AX_X, ALU.add).then_inc(s_part, 1)

                def tail(i, q):
                    position_sum(i, q, x2, s_x2, part2, p2, s_p2)

                run(dve, step, tail, AHEAD_DVE)

            @block.tensor
            def _(pe):
                credit(pe, [(s_tr, TILES), (s_rep1, per_rep1), (s_mm1, per_z1), (s_rep2, per_rep2),
                            (s_hmm, per_u), (s_unit, per_u)])
                pe.wait_ge(s_w, 1)
                pe.wait_ge(s_const, 16 * len(constants))
                pe.wait_ge(s_wl, 2)
                for k in range(C1):
                    mm = nc.tensor.matmul(ps[0:M, BK_ACC1, 0:S], fold_sb[:, k, :], w1_sb[:, k, :], start=(k == 0),
                                          stop=(k == C1 - 1))
                mm.then_inc(s_fold, 1)

                def rep2(i, t, j):
                    jj = J * t + j
                    pe.wait_ge(s_z, at(i, per_u, UNITS * t + 2 * j - 2))
                    nc.tensor.matmul(ps[:, BK_B2[jj % 2], :], sel_r[:, j, :], x0t[:, t % TILES, :],
                                     start=True, stop=True).then_inc(s_rep2, 1)

                def rep1(i, t, k):
                    if k == 0:
                        pe.wait_ge(s_x0t, at(i, TILES, t + 1))
                    pe.wait_ge(s_z1, at(i, per_z1, C1 * t + k - 1))
                    nc.tensor.matmul(ps[0:K1, BK_B1[(C1 * t + k) % 2], :], sel_r[:, J + k, 0:K1],
                                     x0t[:, t % TILES, :], start=True, stop=True).then_inc(s_rep1, 1)

                def layer1(i, t, k):
                    if k == 0:
                        pe.wait_ge(s_x1, at(i, TILES, t))
                        pe.wait_ge(s_w, 3)
                    pe.wait_ge(s_z1, at(i, per_z1, C1 * t + k + 1))
                    K = K1 if k < C1 - 1 else (SHIFTS - SC * (C1 - 1)) * M
                    nc.tensor.matmul(ps[:, BK_ACC1, :], w1_sb[0:K, k, :], z1[0:K, (C1 * t + k) % 2, :],
                                     start=(k == 0), stop=(k == C1 - 1)).then_inc(s_mm1, 1)

                def chunk(u, c):
                    return (u // 2) * G + (u % 2) * UC + c

                def high(i, q, u):
                    w = UNITS * q + u
                    if u == 0:
                        pe.wait_ge(s_x2, at(i, TILES, q - 1))
                    pe.wait_ge(s_h, at(i, per_u, w + 1))
                    for c in range(UC):
                        for weights in (w2h, w2l):
                            mm = nc.tensor.matmul(ps[:, BK_ACC2[q % 2], :], weights[:, chunk(u, c), :],
                                                  hr[:, w % HR, c * N:(c + 1) * N],
                                                  start=(u == 0 and c == 0 and weights is w2h), stop=False)
                    mm.then_inc(s_hmm, 1)

                def finish(i, q, u):
                    w = UNITS * q + u
                    pe.wait_ge(*low_done(i, w))
                    for c in range(UC):
                        mm = nc.tensor.matmul(ps[:, BK_ACC2[q % 2], :], w2h[:, chunk(u, c), :],
                                              lr[:, w % LR, c * N:(c + 1) * N],
                                              start=False, stop=(u == UNITS - 1 and c == UC - 1))
                    mm.then_inc(s_unit, 1)

                def mlp1_start(n, c):
                    end = BLOCKS - 1
                    if n == 0 and c == 0:
                        pe.wait_ge(s_mlpw, 2 * 16)
                        pe.wait_ge(s_x1, at(end, TILES, TILES))
                        pe.wait_ge(s_z1, at(end, per_z1, per_z1))
                        pe.wait_ge(s_x0t, at(end, TILES, TILES))
                    if n == 0:
                        pe.wait_ge(s_part, BLOCKS)
                    else:
                        pe.wait_ge(s_part, 2 * BLOCKS - 1)
                        pe.wait_ge(s_act, MLP.index((1, 0, c)) + 1)
                    cols, f = slice(n * N, (n + 1) * N), slice(c * P, (c + 1) * P)
                    bank = mlp_bank(1, n, c)
                    nc.tensor.matmul(ps[:, bank, :], wt1_sb[:, 0, f], p1[:, cols], start=True, stop=False)
                    nc.tensor.matmul(ps[:, bank, :], wt1c_sb[:, f], ctx_sb[:, cols], start=False, stop=False)

                def mlp(k):
                    layer, n, c = MLP[k]
                    end, bank = BLOCKS - 1, mlp_bank(*MLP[k])
                    if layer == 1:
                        if n == 0:
                            mlp1_start(n, c)
                        else:
                            pe.wait_ge(s_part, 2 * BLOCKS)
                        terms = [(wt1_sb[:, 1, c * P:(c + 1) * P], p2[:, n * N:(n + 1) * N])]
                    elif layer == 2:
                        pe.wait_ge(s_act, MLP.index((1, n, F1 // P - 1)) + 1)
                        if n == 0 and c == 0:
                            pe.wait_ge(s_x2, at(end, TILES, 3))
                        if n == 0 and c == 1:
                            pe.wait_ge(s_z, at(end, per_u, per_u - 2))
                        terms = [(wt2_sb[:, kk, c * P:(c + 1) * P], hidden(1, n, kk)) for kk in range(F1 // P)]
                    else:
                        pe.wait_ge(s_act, MLP.index((2, n, F2 // P - 1)) + 1)
                        if n == 0:
                            pe.wait_ge(s_z, at(end, per_u, per_u))
                        else:
                            pe.wait_ge(s_x2, at(end, TILES, TILES))
                        terms = [(wt3_sb[:, kk:kk + 1], hidden(2, n, kk)) for kk in range(F2 // P)]
                    rows_out = 1 if layer == 3 else P
                    for kk, (w, x) in enumerate(terms):
                        mm = nc.tensor.matmul(ps[0:rows_out, bank, :], w, x, start=(kk == 0 and layer > 1),
                                              stop=(kk == len(terms) - 1))
                    mm.then_inc(s_mlp, 1)

                def step(i, q, u):
                    if there(i, q):
                        if u in (1, 3, 5):
                            rep2(i, q, (u + 3) // 2)
                        high(i, q, u)
                    if u >= LAG and there(i, q):
                        finish(i, q, u - LAG)
                    if u < LAG and there(i, q - 1):
                        finish(i if q else i - 1, (q - 1) % TILES, u - LAG + UNITS)
                    v, ahead = layer1_phase(u)
                    t = q + ahead
                    if there(i, t):
                        if v < C1:
                            rep1(i, t, v)
                        if 1 <= v <= C1:
                            layer1(i, t, v - 1)
                    if u in (7, 9) and there(i, q + 1):
                        rep2(i, q + 1, (u - 7) // 2)
                    if last_lap(i) and q == 2 and u in MLP1_FIRST:
                        mlp(MLP1_FIRST.index(u))
                    if last_lap(i) and q == 3 and u in MLP1_START:
                        mlp1_start(1, MLP1_START.index(u))
                    if u == TRANSPOSE_STEP and there(i, q + 2):
                        if q == 2:
                            pe.wait_ge(s_el, at(i, 1, 2))
                        pe.wait_ge(s_x0t, at(i, TILES, q + 2))
                        for d in range(DT):
                            mm = nc.tensor.transpose(ps[0:2 * M, BK_T, d * P:(d + 1) * P],
                                                     e_hl[:, :, DT * ((q + 2) % TILES) + d], ident_sb[:])
                        mm.then_inc(s_tr, 1)

                def tail(i, q):
                    if last_lap(i) and q == 3:
                        mlp(F1 // P)
                        for u in range(UNITS - LAG, UNITS):
                            finish(i, q, u)

                run(pe, step, tail, AHEAD_PE)

                for k in range(F1 // P + 1, len(MLP)):
                    mlp(k)


def run(eng, step, tail, ahead):
    last = BLOCKS - 1

    def rest(i, q):
        for u in range(ahead, UNITS):
            step(i, q, u)
        if there(i, q + 1):
            for u in range(ahead):
                step(i if q < TILES - 1 else i + 1, (q + 1) % TILES, u)
        tail(i, q)

    for q in range(1, TILES):
        for u in range(UNITS):
            step(-1, q, u)
    for u in range(ahead):
        step(0, 0, u)
    with eng.Fori(0, last) as i:
        for q in range(TILES):
            rest(i, q)
    for q in range(TILES):
        rest(last, q)


def pair_rows():
    k, p = np.meshgrid(np.arange(C1), np.arange(K1), indexing="ij")
    shift, h = SC * k + p // M, p % M
    return h, (h + shift) % M, shift, shift < SHIFTS


def selection():
    sel = np.zeros((2 * M, SEL, P), np.float32)
    for j in range(J):
        for p in range(P):
            if MG * j + p % MG < M:
                sel[MG * j + p % MG, j, p] = 1
    h, m, _, there = pair_rows()
    for p in range(K1):
        for k in range(C1):
            if there[k, p]:
                sel[[h[k, p], m[k, p]], J + k, p] = 1
    sel[M:] = sel[:M]
    return sel


def kernel(**inputs):
    from concourse import bacc
    from concourse.bass_utils import run_bass_kernel_spmd

    x = {k: np.asarray(v) for k, v in inputs.items()}
    w1 = x["L0_rec_W1"]
    h, m, shift, there = pair_rows()
    w1a, w1b = np.zeros((2, K1, C1, S), w1.dtype)
    kk, pp = np.nonzero(there)
    w1a[pp, kk] = w1[:, h[kk, pp], m[kk, pp]].T
    w1b[pp, kk] = w1[:, m[kk, pp], h[kk, pp]].T
    fold = np.zeros((K1, C1, M), np.float32)
    for row in (h, m):
        fold[pp, kk, row[kk, pp]] = np.where(shift[kk, pp] > 0, -1, 1)
    w2 = np.zeros((HG, MG, J, G, S), x["L0_rec_W2"].dtype)
    by = x["L0_rec_W2"].transpose(1, 2, 0).reshape(G, HG, M, S)
    for j in range(J):
        mm = range(MG * j, min(MG * j + MG, M))
        w2[:, :len(mm), j] = by[:, :, mm.start:mm.stop].transpose(1, 2, 0, 3)
    w2 = w2.reshape(P, CHUNKS, S)
    arrays = {
        "ids": x["ids"],
        "w1a": w1a, "w1b": w1b, "b1": x["L0_rec_b1"].reshape(S, 1), "fold": fold,
        "w2": w2,
        "b2": x["L0_rec_b2"].reshape(S, 1),
        "sel": selection(), "ident": np.eye(P, dtype=np.float32),
        "wt1": x["W_top1"][:2 * S].reshape(2, S, F1).transpose(1, 0, 2), "wt1c": x["W_top1"][2 * S:],
        "bt1": x["b_top1"].reshape(F1 // P, P).T,
        "wt2": x["W_top2"].reshape(F1 // P, P, F2).transpose(1, 0, 2),
        "bt2": x["b_top2"].reshape(F2 // P, P).T,
        "wt3": x["W_top3"].reshape(F2 // P, P).T,
        "ctx_t": x["dense_ctx"].T,
    }
    tables = {f"tbl_{f}": x[f"tbl_{f}"] for f in range(M)}
    nc = bacc.Bacc("TRN2", target_bir_lowering=False, num_devices=1)
    data, aps = {}, {}
    for name, a in {**arrays, **tables}.items():
        data[f"in_{name}"] = np.ascontiguousarray(a)
        aps[name] = nc.dram_tensor(f"in_{name}", a.shape, mybir.dt.from_np(a.dtype), kind="ExternalInput").ap()
    out = nc.dram_tensor("out_y", (B, 1), F32, kind="ExternalOutput").ap()
    cin_tower(nc, [aps[f"tbl_{f}"] for f in range(M)], **{k: aps[k] for k in arrays},
              out=out.rearrange("b o -> o b"))
    r = run_bass_kernel_spmd(nc, [data], core_ids=[0])
    return r.results[0]["out_y"]
```
